# Optimizing a Trainium2 kernel written in Bass

```python
import numpy as np
import jax
import jax.numpy as jnp

def _softmax(x, axis=-1):
    return jax.nn.softmax(x, axis=axis)

def _gelu(x):
    return jax.nn.gelu(x, approximate=True)

def _silu(x):
    return jax.nn.silu(x)

def _sigmoid(x):
    return jax.nn.sigmoid(x)

def _layernorm(x, axis=-1, eps=1e-05):
    m = jnp.mean(x, axis=axis, keepdims=True)
    v = jnp.var(x, axis=axis, keepdims=True)
    return (x - m) / jnp.sqrt(v + eps)

def _scatter_add(tgt, idx, src, axis=0):
    return tgt.at[idx].add(src)

def _segment_sum(src, seg, n):
    return jax.ops.segment_sum(src, seg, n)
kernel_name = 'mk_recurrent_d1_jaxref_r8_604d7a'

def setup_inputs(seed: int=0):
    np.random.seed(seed)
    _w = jnp.asarray

    def _L0_attn_setup():
        import jax, jax.numpy as jnp
        import numpy as np
        DIM = 128
        DEPTH = 6
        HEADS = 8
        FF_MULT = 4
        LN_EPS = 1e-05
        LEAKY_SLOPE = 0.01

        def _layernorm(x, w, b):
            m = jnp.mean(x, axis=-1, keepdims=True)
            v = jnp.mean(jnp.square(x - m), axis=-1, keepdims=True)
            return (x - m) * jax.lax.rsqrt(v + LN_EPS) * w + b

        def _linear_attn(q, k, v):
            q = jax.nn.softmax(q, axis=-1)
            k = jax.nn.softmax(k, axis=-2)
            context = jnp.einsum('bhnd,bhne->bhde', k, v)
            return jnp.einsum('bhnd,bhde->bhne', q, context)
        key = jax.random.key(seed)
        ks = jax.random.split(key, 12)
        b, t = (2, 512)
        s = 0.02
        return {'x': jax.random.normal(ks[0], (b, t, DIM), dtype=jnp.float32), 'ln1_w': jnp.ones((DEPTH, DIM), jnp.float32), 'ln1_b': jnp.zeros((DEPTH, DIM), jnp.float32), 'wq': jax.random.normal(ks[1], (DEPTH, DIM, DIM), jnp.float32) * s, 'wk': jax.random.normal(ks[2], (DEPTH, DIM, DIM), jnp.float32) * s, 'wv': jax.random.normal(ks[3], (DEPTH, DIM, DIM), jnp.float32) * s, 'wo': jax.random.normal(ks[4], (DEPTH, DIM, DIM), jnp.float32) * s, 'bo': jnp.zeros((DEPTH, DIM), jnp.float32), 'ln2_w': jnp.ones((DEPTH, DIM), jnp.float32), 'ln2_b': jnp.zeros((DEPTH, DIM), jnp.float32), 'w1': jax.random.normal(ks[5], (DEPTH, DIM, FF_MULT * DIM), jnp.float32) * s, 'w2': jax.random.normal(ks[6], (DEPTH, FF_MULT * DIM, DIM), jnp.float32) * s}
    _L0_attn_in = _L0_attn_setup()

    def _L0_ffn_setup():
        import jax, jax.numpy as jnp
        import numpy as np
        B, S, D, E = (2, 256, 128, 8)
        key = jax.random.key(seed)
        ks = jax.random.split(key, 5)
        x = jax.random.normal(ks[0], (B, S, D), dtype=jnp.float32)
        router_w = jax.random.normal(ks[1], (E, D), dtype=jnp.float32) * 0.02
        router_b = jnp.zeros((E,), dtype=jnp.float32)
        expert_w = jax.random.normal(ks[2], (E, D, D), dtype=jnp.float32) * 0.02
        expert_b = jnp.zeros((E, D), dtype=jnp.float32)
        return {'x': x, 'router_w': router_w, 'router_b': router_b, 'expert_w': expert_w, 'expert_b': expert_b}
    _L0_ffn_in = _L0_ffn_setup()
    _d = {'L0_attn_x': _L0_attn_in['x'], 'L0_attn_ln1_w': _L0_attn_in['ln1_w'], 'L0_attn_ln1_b': _L0_attn_in['ln1_b'], 'L0_attn_wq': _L0_attn_in['wq'], 'L0_attn_wk': _L0_attn_in['wk'], 'L0_attn_wv': _L0_attn_in['wv'], 'L0_attn_wo': _L0_attn_in['wo'], 'L0_attn_bo': _L0_attn_in['bo'], 'L0_attn_ln2_w': _L0_attn_in['ln2_w'], 'L0_attn_ln2_b': _L0_attn_in['ln2_b'], 'L0_attn_w1': _L0_attn_in['w1'], 'L0_attn_w2': _L0_attn_in['w2'], 'L0_ffn_router_w': _L0_ffn_in['router_w'], 'L0_ffn_router_b': _L0_ffn_in['router_b'], 'L0_ffn_expert_w': _L0_ffn_in['expert_w'], 'L0_ffn_expert_b': _L0_ffn_in['expert_b']}
    _x0 = _d['L0_attn_x']
    _d['L0_attn_x'] = jax.random.normal(jax.random.fold_in(jax.random.key(seed), 1), (4, 1024, 128), dtype=_x0.dtype)
    del _x0
    return _d

def reference(L0_attn_x, L0_attn_ln1_w, L0_attn_ln1_b, L0_attn_wq, L0_attn_wk, L0_attn_wv, L0_attn_wo, L0_attn_bo, L0_attn_ln2_w, L0_attn_ln2_b, L0_attn_w1, L0_attn_w2, L0_ffn_router_w, L0_ffn_router_b, L0_ffn_expert_w, L0_ffn_expert_b):

    def _L0_attn_ref(x, ln1_w, ln1_b, wq, wk, wv, wo, bo, ln2_w, ln2_b, w1, w2):
        import jax, jax.numpy as jnp
        import numpy as np
        DIM = 128
        DEPTH = 6
        HEADS = 8
        FF_MULT = 4
        LN_EPS = 1e-05
        LEAKY_SLOPE = 0.01

        def _layernorm(x, w, b):
            m = jnp.mean(x, axis=-1, keepdims=True)
            v = jnp.mean(jnp.square(x - m), axis=-1, keepdims=True)
            return (x - m) * jax.lax.rsqrt(v + LN_EPS) * w + b

        def _linear_attn(q, k, v):
            q = jax.nn.softmax(q, axis=-1)
            k = jax.nn.softmax(k, axis=-2)
            context = jnp.einsum('bhnd,bhne->bhde', k, v)
            return jnp.einsum('bhnd,bhde->bhne', q, context)
        b, t, e = x.shape
        h, dh = (HEADS, e // HEADS)
        for i in range(DEPTH):
            xn = _layernorm(x, ln1_w[i], ln1_b[i])
            q = (xn @ wq[i]).reshape(b, t, h, dh).transpose(0, 2, 1, 3)
            k = (xn @ wk[i]).reshape(b, t, h, dh).transpose(0, 2, 1, 3)
            v = (xn @ wv[i]).reshape(b, t, h, dh).transpose(0, 2, 1, 3)
            attn = _linear_attn(q, k, v)
            attn = attn.transpose(0, 2, 1, 3).reshape(b, t, e)
            x = attn @ wo[i] + bo[i] + x
            xn = _layernorm(x, ln2_w[i], ln2_b[i])
            hdn = xn @ w1[i]
            hdn = jnp.where(hdn >= 0, hdn, LEAKY_SLOPE * hdn)
            x = hdn @ w2[i] + x
        return x

    def _L0_ffn_ref(x, router_w, router_b, expert_w, expert_b):
        import jax, jax.numpy as jnp
        import numpy as np
        B, S, D, E = (2, 256, 128, 8)
        logits = jnp.einsum('bsd,ed->bse', x, router_w) + router_b
        probs = jax.nn.softmax(logits, axis=-1)
        weights = jnp.max(probs, axis=-1)
        top1 = jnp.argmax(probs, axis=-1)
        y_all = jnp.einsum('bsd,eod->bseo', x, expert_w) + expert_b
        y = jnp.take_along_axis(y_all, top1[:, :, None, None], axis=2)[:, :, 0, :]
        out = y * weights[:, :, None]
        return out
    x = L0_attn_x
    xn = _layernorm(x, axis=-1)
    s = _L0_attn_ref(xn, L0_attn_ln1_w, L0_attn_ln1_b, L0_attn_wq, L0_attn_wk, L0_attn_wv, L0_attn_wo, L0_attn_bo, L0_attn_ln2_w, L0_attn_ln2_b, L0_attn_w1, L0_attn_w2)
    g = _silu(_L0_ffn_ref(xn, L0_ffn_router_w, L0_ffn_router_b, L0_ffn_expert_w, L0_ffn_expert_b))
    x = x + s * g
    return x

_drawn_inputs = setup_inputs


def setup_inputs(seed=0):
    import zlib

    import numpy as np

    out = dict(_drawn_inputs(seed))
    spreads = {'L0_attn_ln1_w': (1.0, 0.6),
     'L0_attn_ln1_b': (0.0, 0.8),
     'L0_attn_bo': (0.0, 0.8),
     'L0_attn_ln2_w': (1.0, 0.6),
     'L0_attn_ln2_b': (0.0, 0.8),
     'L0_ffn_router_b': (0.0, 0.595),
     'L0_ffn_expert_b': (0.0, 0.8)}
    factors = {'L0_attn_wq': 8.0,
     'L0_attn_wk': 8.0,
     'L0_attn_wv': 8.0,
     'L0_attn_wo': 8.0,
     'L0_attn_w1': 8.0,
     'L0_attn_w2': 8.0,
     'L0_ffn_router_w': 2.734,
     'L0_ffn_expert_w': 2.686}
    for name, (base, spread) in spreads.items():
        noise = np.random.default_rng([zlib.crc32(name.encode()), seed]).standard_normal(out[name].shape)
        drawn = base * np.exp(spread * noise) if base else spread * noise
        out[name] = jnp.asarray(drawn.astype(out[name].dtype))
    for name, factor in factors.items():
        out[name] = (out[name] * factor).astype(out[name].dtype)
    return out
```

```python
from contextlib import ExitStack

import concourse.bass as bass
from concourse import mybir

ALU = mybir.AluOpType
ACT = mybir.ActivationFunctionType
AX_X = mybir.AxisListType.X
F32 = mybir.dt.float32
F32R = mybir.dt.float32r
I32 = mybir.dt.int32

EPS = 1e-5
SLOPE = 0.01


def build_program(nc, x_in, ln_params, wq, wk, wv, wo, bo, w1, w2, router_wT, router_b, expert_wT, expert_b, out):
    NBATCH, T, D = x_in.shape
    L = wq.shape[0]
    FF = w1.shape[2]
    E = router_wT.shape[1]
    H = 8
    DH = D // H
    P = 128
    NT = T // P
    HALF = T // 2
    NC = FF // P
    NF = 2 * NC
    assert NBATCH == 4 and D == P and NT == 8 and NC == 4 and E == 8

    with ExitStack() as ctx:
        def sb(name, shape, dt=F32):
            return ctx.enter_context(nc.sbuf_tensor(name, shape, dt))

        def ps(name, shape):
            return ctx.enter_context(nc.psum_tensor(name, shape, F32))

        def sem(name):
            return ctx.enter_context(nc.semaphore(name))

        psT = ps("psT", [P, T])
        psM = ps("psM", [P, T])
        psY = ps("psY", [P, HALF])
        psS = ps("psS", [P, HALF])
        psH = ps("psH", [P, 2, HALF])

        xraw = sb("xraw", [P, NBATCH, T])
        X = sb("X", [P, NBATCH, T])
        gate = sb("gate", [P, NBATCH, T])
        wq_all = sb("wq_all", [P, L, D])
        wk_all = sb("wk_all", [P, L, D])
        wv_all = sb("wv_all", [P, L, D])
        wo_all = sb("wo_all", [P, L, D])
        w1_all = sb("w1_all", [P, L, FF])
        w2_all = sb("w2_all", [P, L, NC, D])
        lnp = sb("lnp", [P, 4, L])
        lns = sb("lns", [P, 4])
        bo_row = sb("bo_row", [1, L, D])
        wk_s = sb("wk_s", [P, D])
        wv_s = sb("wv_s", [P, D])
        w1_hi = sb("w1_hi", [P, NC, P], F32R)
        w1_lo = sb("w1_lo", [P, NC, P], F32R)
        ident = sb("ident", [P, P])
        head_mask = sb("head_mask", [P, P])
        ones = sb("ones", [P, P])
        eighth = sb("eighth", [1, P])
        minus_half = sb("minus_half", [P, NT])
        rank = sb("rank", [P, E])
        st = sb("st", [P, NT, 6])
        sdiff = sb("sdiff", [P, NT])
        sdev = sb("sdev", [P, NT])
        mean = sb("mean", [P, 2, 2, NT])
        veps = sb("veps", [P, 2, 2, NT])
        rstd = sb("rstd", [P, 2, 2, NT])
        shift2 = sb("shift2", [P, NT])
        xh1 = sb("xh1", [P, 2, T])
        xnT = sb("xnT", [P, T])
        negkmax = sb("negkmax", [P, 2])
        ksum = sb("ksum", [P, 2])
        krec = sb("krec", [P, 1])
        expk = sb("expk", [P, T])
        expkT = sb("expkT", [P, T])
        qmax = sb("qmax", [P, NT * H])
        qsum = sb("qsum", [P, NT * H])
        qrec = sb("qrec", [P, NT * H])
        qe = sb("qe", [P, T])
        qsm = sb("qsm", [P, T])
        qsmT = sb("qsmT", [P, T])
        gT = sb("gT", [P, D])
        ctxT = sb("ctxT", [P, D])
        mix = sb("mix", [P, D])
        bvm = sb("bvm", [P, D])
        bias_row = sb("bias_row", [P, D])
        xh2 = sb("xh2", [P, T])
        xn2 = sb("xn2", [P, T])
        xn2_hi = sb("xn2_hi", [P, T], F32R)
        xn2_lo = sb("xn2_lo", [P, T], F32R)
        hsl = sb("hsl", [P, 2, HALF])
        hid = sb("hid", [P, NC, HALF])
        ewn = sb("ewn", [P, E, D])
        ew_hi = sb("ew_hi", [P, E, D], F32R)
        ew_lo = sb("ew_lo", [P, E, D], F32R)
        rwT = sb("rwT", [P, E])
        rb_bc = sb("rb_bc", [P, E])
        eb_diag = sb("eb_diag", [NT * E, NT, D])
        lg = sb("lg", [P, NT, E])
        lmax = sb("lmax", [P, NT])
        eq = sb("eq", [P, NT, E])
        lmax2 = sb("lmax2", [P, NT])
        pick = sb("pick", [P, NT, E])
        le = sb("le", [P, NT, E])
        lsum = sb("lsum", [P, NT])
        lrec = sb("lrec", [P, NT])
        pickT = sb("pickT", [NT * E, P])
        ebuf = sb("ebuf", [P, 2, E, D])

        S = {}

        def sig(name):
            if name not in S:
                S[name] = sem(name)
            return S[name]

        def wait(eng, name, value):
            if isinstance(value, int) and value <= 0:
                return
            eng.wait_ge(sig(name), value)

        def tile(a, t):
            return a[:, t * P:(t + 1) * P]

        def by_head(a):
            return a.rearrange("p (g d) -> p g d", d=DH)

        def over_head(a):
            return a.unsqueeze(2).broadcast_to([P, NT * H, DH])

        def xb(a, b, lo=0, n=T):
            if isinstance(b, int):
                return a[:, b, lo:lo + n]
            return a[:, :, :].rearrange("p b t -> p (b t)")[:, bass.ds(b * T + lo, n)]

        def of_layer(a, l, lo, n):
            flat = a[:, :, :, :].rearrange("p l c d -> p (l c d)") if len(a.shape) == 4 \
                else a[:, :, :].rearrange("p l d -> p (l d)")
            w = flat.shape[1] // L
            if isinstance(l, int):
                return flat[:, l * w + lo:l * w + lo + n]
            return flat[:, bass.ds(l * w + lo, n)]

        def param(k, l):
            if isinstance(l, int):
                return lnp[:, k, l:l + 1]
            return lnp[:, k, bass.ds(l, 1)]

        def batches(eng, body):
            body(0)
            with eng.Fori(1, NBATCH) as b:
                body(b)

        def slots(eng, slot):
            for j in range(4):
                slot(0, j)
            with eng.Fori(1, L) as l:
                for j in range(4):
                    slot(l, j)
            for j in range(2):
                slot(L, j)

        def items(l, j):
            def there(lag):
                if isinstance(l, int):
                    n = 4 * l + j - lag
                    return 0 <= n < 4 * L
                return True
            return (there(0), l), (there(1), l if j >= 1 else l - 1), (there(2), l if j >= 2 else l - 1)

        block = ctx.enter_context(nc.Block())

        @block.sync
        def _(sp):
            for b in range(NBATCH):
                sp.dma_start(xraw[:, b, :], x_in[b].rearrange("(p t) d -> p (t d)", p=P)) \
                    .then_inc(sig("x_loaded"), 16)
                if b == 0:
                    sp.dma_start(rb_bc[:, :], router_b.rearrange("(a e) -> a e", a=1).broadcast_to([P, E])) \
                        .then_inc(sig("router_loaded"), 16)
                    sp.dma_start(ewn[:, :, :], expert_wT) \
                        .then_inc(sig("expert_loaded"), 16)
            for l in range(L):
                sp.dma_start(wk_all[:, l, :], wk[l]).then_inc(sig("attn_loaded"), 16)
                sp.dma_start(wq_all[:, l, :], wq[l]).then_inc(sig("attn_loaded"), 16)
                sp.dma_start(wv_all[:, l, :], wv[l]).then_inc(sig("attn_loaded"), 16)
                sp.dma_start(wo_all[:, l, :], wo[l]).then_inc(sig("attn_loaded"), 16)
                sp.dma_start(w1_all[:, l, :], w1[l]).then_inc(sig("ffn_loaded"), 16)
                sp.dma_start(w2_all[:, l, :, :], w2[l].rearrange("(p c) d -> p c d", c=NC)) \
                    .then_inc(sig("ffn_loaded"), 16)
            for b in range(NBATCH):
                sp.wait_ge(sig("out_ready"), b + 1)
                sp.dma_start(out[b].rearrange("(p t) d -> p (t d)", p=P), xraw[:, b, :]) \
                    .then_inc(sig("stored"), 16)
            sp.wait_ge(sig("stored"), 16 * NBATCH)

        @block.tensor
        def _(pe):
            def transposes(dst, src):
                for t in range(NT):
                    last = nc.tensor.transpose(tile(dst, t), tile(src, t), ident[:, :])
                return last

            def split_product(dst, hi_w, lo_w, hi_x, lo_x):
                nc.tensor.matmul(dst, hi_w, hi_x, start=True, stop=False)
                nc.tensor.matmul(dst, lo_w, hi_x, start=False, stop=False)
                return nc.tensor.matmul(dst, hi_w, lo_x, start=False, stop=True)

            pe.wait_ge(sig("const_ready"), 5)
            def expert_batch(b):
                wait(pe, "xh0_ready", b + 1)
                wait(pe, "xn0T_ready", b)
                transposes(psT, xh1[:, 0, :]).then_inc(sig("t0_done"), 1)
                wait(pe, "xn0T_ready", b + 1)
                pe.wait_ge(sig("router_loaded"), 32)
                wait(pe, "z_ready", b)
                for t in range(NT):
                    last = nc.tensor.matmul(psS[:, t * E:(t + 1) * E], tile(xnT, t), rwT[:, :],
                                            start=True, stop=True)
                last.then_inc(sig("logits_done"), 1)
                wait(pe, "xn0_split", b + 1)
                pe.wait_ge(sig("ew_split"), 1)
                for t in range(NT):
                    for h in range(2):
                        wait(pe, "picked", 2 * NT * b + 2 * t + h - 1 if t else 2 * NT * b)
                        last = split_product(psM[:, h * HALF:(h + 1) * HALF], tile(xn2_hi, t), tile(xn2_lo, t),
                                             ew_hi[:, 4 * h:4 * h + 4, :], ew_lo[:, 4 * h:4 * h + 4, :])
                        last.then_inc(sig("experts_done"), 1)
                pe.wait_ge(sig("const_ready"), 5)
                wait(pe, "pick_ready", b + 1)
                nc.tensor.transpose(psY[0:NT * E, 0:P], pick[:, :, :].rearrange("p t e -> p (t e)"), ident[:, :]) \
                    .then_inc(sig("pickT_done"), 1)
                wait(pe, "pickT_ready", b + 1)
                pe.wait_ge(sig("eb_loaded"), 16 * NT)
                for h in range(2):
                    for t in range(4):
                        last = nc.tensor.matmul(psH[:, h, t * P:(t + 1) * P], pickT[:, :],
                                                eb_diag[:, 4 * h + t, :], start=True, stop=True)
                last.then_inc(sig("ebias_done"), 1)

            batches(pe, expert_batch)

            def w1_step(f, i):
                half, c = i // NC, i % NC
                if i == 0:
                    wait(pe, "xn2_lo_ready", f + 1)
                wait(pe, "hid_ready", NF * f + i - 1)
                cols = slice(half * HALF, (half + 1) * HALF)
                split_product(psH[:, i % 2, :], w1_hi[:, c, :], w1_lo[:, c, :], xn2_hi[:, cols], xn2_lo[:, cols]) \
                    .then_inc(sig("h_done"), 1)

            def w2_step(f, l, i):
                c = i % NC
                wait(pe, "hid_ready", NF * f + i + 1)
                if c == 0:
                    wait(pe, "y_added", 2 * f + i // NC)
                for t in range(4):
                    last = nc.tensor.matmul(tile(psY, t), tile(hid[:, i % NC, :], t), of_layer(w2_all, l, c * D, D),
                                            start=(c == 0 and t == 0), stop=(c == NC - 1), skip_group_check=True)
                if c == NC - 1:
                    last.then_inc(sig("y_done"), 1)

            def slot(l, j):
                (attn, _), (norm2, _), (ffn, lf) = items(l, j)
                n = 4 * l + j
                f = n - 2

                def ffn_step(i):
                    if ffn:
                        if i < NF:
                            if i == 0 and j == 2:
                                wait(pe, "w1_staged", l + 1)
                            w1_step(f, i)
                        if i >= 2:
                            w2_step(f, lf, i - 2)

                if attn:
                    wait(pe, "xh1_ready", NT * (n + 1))
                    wait(pe, "xn2_ready", n - 1)
                    transposes(psT, xh1[:, j % 2, :]).then_inc(sig("t1_done"), 1)
                ffn_step(0)
                ffn_step(1)
                if attn:
                    wait(pe, "xnT_ready", n + 1)
                    if j == 0:
                        wait(pe, "wkv_staged", l + 1)
                    for h in (0, 1):
                        last = nc.tensor.matmul(psT[:, h * HALF:(h + 1) * HALF], wk_s[:, :],
                                                xnT[:, h * HALF:(h + 1) * HALF], start=True, stop=True)
                    last.then_inc(sig("k_done"), 1)
                    wait(pe, "x1_added", n)
                    for t in range(NT):
                        last = nc.tensor.matmul(tile(psM, t), tile(xnT, t), of_layer(wq_all, l, 0, D),
                                                start=True, stop=True)
                    last.then_inc(sig("q_done"), 1)
                    if j == 0:
                        wait(pe, "mix_ready", n)
                        nc.tensor.matmul(psS[:, 0:1], wv_s[:, :], lns[:, 1:2], start=True, stop=True) \
                            .then_inc(sig("bv_done"), 1)
                ffn_step(2)
                if attn:
                    wait(pe, "expk_ready", n + 1)
                    transposes(psT, expk).then_inc(sig("tk_done"), 1)
                    if j == 0:
                        wait(pe, "bv_ready", l + 1)
                        nc.tensor.matmul(psS[:, 0:D], bvm[:, :], of_layer(wo_all, l, 0, D), start=True, stop=False)
                        nc.tensor.matmul(psS[:, 0:D], eighth[:, :], of_layer(bo_row, l, 0, D),
                                         start=False, stop=True).then_inc(sig("bias_done"), 1)
                ffn_step(3)
                ffn_step(4)
                if attn:
                    wait(pe, "expkT_ready", n + 1)
                    wait(pe, "mix_ready", n)
                    wait(pe, "bias_ready", l + 1)
                    for t in range(NT):
                        last = nc.tensor.matmul(psS[:, 0:D], tile(xh1[:, j % 2, :], t), tile(expkT, t),
                                                start=(t == 0), stop=(t == NT - 1))
                    last.then_inc(sig("g_done"), 1)
                ffn_step(5)
                if attn:
                    wait(pe, "gT_ready", n + 1)
                    nc.tensor.matmul(psS[:, 0:D], wv_s[:, :], gT[:, :], start=True, stop=True) \
                        .then_inc(sig("ctx_done"), 1)
                    wait(pe, "qsm_ready", n + 1)
                    transposes(psT, qsm).then_inc(sig("tq_done"), 1)
                ffn_step(6)
                if attn:
                    wait(pe, "ctx_ready", n + 1)
                    nc.tensor.matmul(psS[:, 0:D], ctxT[:, :], of_layer(wo_all, l, 0, D), start=True, stop=True) \
                        .then_inc(sig("mix_done"), 1)
                ffn_step(7)
                if norm2:
                    wait(pe, "xh2_ready", NT * n)
                    if attn:
                        wait(pe, "qsmT_ready", n + 1)
                    transposes(psT, xh2).then_inc(sig("t2_done"), 1)
                if attn:
                    wait(pe, "mix_ready", n + 1)
                    wait(pe, "qsmT_ready", n + 1)
                    wait(pe, "qe_ready", n + 1)
                    for t in range(NT):
                        last = nc.tensor.matmul(tile(psM, t), tile(qsmT, t), mix[:, :], start=True, stop=True)
                    last.then_inc(sig("attn_done"), 1)
                ffn_step(8)
                ffn_step(9)

            wait(pe, "ffn_loaded", 16 * 2 * L)
            wait(pe, "attn_loaded", 16 * 4 * L)
            wait(pe, "param_loaded", 16 * 2)
            wait(pe, "ones_ready", 1)
            wait(pe, "z_ready", NBATCH)
            slots(pe, slot)

        @block.scalar
        def _(act):
            act.dma_start(rwT[:, :], router_wT).then_inc(sig("router_loaded"), 16)
            act.dma_start(lnp[:, :, :], ln_params).then_inc(sig("param_loaded"), 16)
            act.dma_start(bo_row[:, :, :], bo.rearrange("l (a d) -> a l d", a=1)).then_inc(sig("param_loaded"), 16)

            act.wait_ge(sig("expert_loaded"), 16)
            nc.scalar.activation(ew_hi[:, :, :], ewn[:, :, :], ACT.Copy) \
                .then_inc(sig("ew_hi_ready"), 1)
            def router_batch(b):
                wait(act, "t0_done", b + 1)
                nc.scalar.activation(xnT[:, :], psT[:, :], ACT.Copy).then_inc(sig("xn0T_ready"), 1)
                nc.scalar.activation(xb(X, b), xh1[:, 0, :], ACT.Copy).then_inc(sig("x0_ready"), 1)
                wait(act, "lsub_ready", b + 1)
                nc.scalar.activation(le[:, :, :], lg[:, :, :], ACT.Exp).then_inc(sig("lexp_ready"), 1)

            batches(act, router_batch)
            def gate_batch(b):
                wait(act, "z_ready", b + 1)
                nc.scalar.activation(xb(gate, b), xb(gate, b), ACT.Silu).then_inc(sig("gate_ready"), 1)

            batches(act, gate_batch)

            def slot(l, j):
                (attn, _), (norm2, lm), (ffn, _) = items(l, j)
                n = 4 * l + j
                f = n - 2

                def slope(i):
                    if ffn:
                        wait(act, "h_done", NF * f + i + 1)
                        nc.scalar.activation(hsl[:, i % 2, :], psH[:, i % 2, :], ACT.Copy, scale=SLOPE) \
                            .then_inc(sig("hsl_ready"), 1)

                if attn:
                    wait(act, "t1_done", n + 1)
                    wait(act, "q_done", n)
                    if j == 0:
                        wait(act, "wkv_staged", l + 1)
                    nc.scalar.activation(xnT[:, :], psT[:, :], ACT.Identity, bias=lns[:, 1:2], scale=lns[:, 0:1]) \
                        .then_inc(sig("xnT_ready"), 1)
                slope(0)
                slope(1)
                if attn:
                    wait(act, "negkmax_ready", n + 1)
                    nc.scalar.activation(expk[:, :], psT[:, :], ACT.Exp, bias=negkmax[:, j % 2:j % 2 + 1],
                                         accum_out=ksum[:, j % 2:j % 2 + 1]).then_inc(sig("expk_ready"), 1)
                slope(2)
                if attn:
                    wait(act, "tk_done", n + 1)
                    nc.scalar.activation(expkT[:, :], psT[:, :], ACT.Copy).then_inc(sig("expkT_ready"), 1)
                    wait(act, "qe_ready", n + 1)
                    nc.scalar.activation(qe[:, :], qe[:, :], ACT.Exp).then_inc(sig("expq_ready"), 1)
                slope(3)
                slope(4)
                if norm2:
                    wait(act, "shift2_ready", n)
                    wait(act, "t2_done", n - 1)
                    for t in range(NT):
                        nc.scalar.activation(tile(xh2, t), xb(X, (j - 1) % 4, t * P, P), ACT.Identity,
                                             bias=shift2[:, t:t + 1], scale=rstd[:, 1, 0, t:t + 1]) \
                            .then_inc(sig("xh2_ready"), 1)
                slope(5)
                if attn:
                    wait(act, "tq_done", n + 1)
                    nc.scalar.activation(qsmT[:, :], psT[:, :], ACT.Copy).then_inc(sig("qsmT_ready"), 1)
                slope(6)
                slope(7)
                if norm2:
                    wait(act, "t2_done", n)
                    wait(act, "xn2_lo_ready", n - 1)
                    if j == 1:
                        wait(act, "ln2_staged", l + 1)
                    nc.scalar.activation(xn2[:, :], psT[:, :], ACT.Identity, bias=lns[:, 3:4], scale=lns[:, 2:3]) \
                        .then_inc(sig("xn2_ready"), 1)

            slots(act, slot)

        @block.vector
        def _(dve):
            def tile_statistics(src, name):
                for t in range(NT):
                    last = nc.vector.bn_stats(st[:, t, :], src(t))
                last.then_inc(sig(name + "_st"), 1)

            def token_statistics(norm, par, name, count):
                wait(dve, name + "_st", count)
                nc.vector.tensor_tensor(mean[:, norm, par, :], st[:, :, 1], st[:, :, 4], ALU.add)
                nc.vector.tensor_tensor(sdiff[:, :], st[:, :, 1], st[:, :, 4], ALU.subtract)
                nc.vector.tensor_tensor(sdev[:, :], st[:, :, 2], st[:, :, 5], ALU.add).then_inc(sig(name + "_sum"), 1)
                wait(dve, name + "_sum", count)
                nc.vector.tensor_tensor(sdiff[:, :], sdiff[:, :], sdiff[:, :], ALU.mult)
                nc.vector.tensor_scalar(mean[:, norm, par, :], mean[:, norm, par, :], -0.5 if norm == 1 else 0.5, None,
                                        ALU.mult)
                nc.vector.tensor_scalar(sdev[:, :], sdev[:, :], 1.0 / D, EPS, ALU.mult, ALU.add) \
                    .then_inc(sig(name + "_sq"), 1)
                wait(dve, name + "_sq", count)
                nc.vector.scalar_tensor_tensor(veps[:, norm, par, :], sdiff[:, :], 0.25, sdev[:, :],
                                               ALU.mult, ALU.add).then_inc(sig(name + "_var"), 1)

            dve.wait_ge(sig("ew_hi_ready"), 1)
            nc.vector.tensor_tensor(ew_lo[:, :, :], ewn[:, :, :], ew_hi[:, :, :].bitcast(F32), ALU.subtract) \
                .then_inc(sig("ew_split"), 1)
            nc.vector.memset(ones[:, :], 1.0)
            nc.vector.memset(eighth[:, :], 1.0 / H).then_inc(sig("ones_ready"), 1)
            dve.wait_ge(sig("ones_ready"), 1)
            dve.wait_ge(sig("mask_ready"), 1)
            dve.wait_ge(sig("rank_ready"), E)
            dve.wait_ge(sig("x_loaded"), 16 * NBATCH)
            dve.wait_ge(sig("router_loaded"), 32)
            def expert_batch(b):
                tile_statistics(lambda t: xb(xraw, b, t * P, P), "n0")
                token_statistics(0, 0, "n0", b + 1)
                wait(dve, "n0_rstd", b + 1)
                wait(dve, "t0_done", b)
                wait(dve, "x0_ready", b)
                for t in range(NT):
                    last = nc.vector.tensor_scalar(tile(xh1[:, 0, :], t), xb(xraw, b, t * P, P),
                                                   mean[:, 0, 0, t:t + 1], rstd[:, 0, 0, t:t + 1],
                                                   ALU.subtract, ALU.mult)
                last.then_inc(sig("xh0_ready"), 1)
                wait(dve, "xn0T_ready", b + 1)
                nc.vector.tensor_copy(xn2_hi[:, :], xnT[:, :]).then_inc(sig("xn0_hi_ready"), 1)
                wait(dve, "logits_done", b + 1)
                nc.vector.tensor_tensor(lg[:, :, :], psS[:, 0:NT * E].rearrange("p (t e) -> p t e", e=E),
                                        rb_bc[:, :].unsqueeze(1).broadcast_to([P, NT, E]), ALU.add) \
                    .then_inc(sig("lg_ready"), 1)
                wait(dve, "lg_ready", b + 1)
                nc.vector.tensor_reduce(lmax[:, :], lg[:, :, :], AX_X, ALU.max).then_inc(sig("lmax_ready"), 1)
                wait(dve, "lmax_ready", b + 1)
                nc.vector.tensor_tensor(eq[:, :, :], lg[:, :, :],
                                        lmax[:, :].unsqueeze(2).broadcast_to([P, NT, E]), ALU.is_equal) \
                    .then_inc(sig("eq_ready"), 1)
                nc.vector.tensor_tensor(lg[:, :, :], lg[:, :, :],
                                        lmax[:, :].unsqueeze(2).broadcast_to([P, NT, E]), ALU.subtract) \
                    .then_inc(sig("lsub_ready"), 1)
                wait(dve, "eq_ready", b + 1)
                nc.vector.tensor_tensor(eq[:, :, :], eq[:, :, :],
                                        rank[:, :].unsqueeze(1).broadcast_to([P, NT, E]), ALU.mult) \
                    .then_inc(sig("score_ready"), 1)
                wait(dve, "score_ready", b + 1)
                nc.vector.tensor_reduce(lmax2[:, :], eq[:, :, :], AX_X, ALU.max).then_inc(sig("lmax2_ready"), 1)
                wait(dve, "lexp_ready", b + 1)
                nc.vector.tensor_reduce(lsum[:, :], le[:, :, :], AX_X, ALU.add).then_inc(sig("lsum_ready"), 1)
                wait(dve, "lsum_ready", b + 1)
                nc.vector.reciprocal(lrec[:, :], lsum[:, :]).then_inc(sig("lrec_ready"), 1)
                wait(dve, "lmax2_ready", b + 1)
                nc.vector.tensor_tensor(pick[:, :, :], eq[:, :, :],
                                        lmax2[:, :].unsqueeze(2).broadcast_to([P, NT, E]), ALU.is_equal) \
                    .then_inc(sig("first_ready"), 1)
                wait(dve, "first_ready", b + 1)
                wait(dve, "lrec_ready", b + 1)
                nc.vector.tensor_tensor(pick[:, :, :], pick[:, :, :],
                                        lrec[:, :].unsqueeze(2).broadcast_to([P, NT, E]), ALU.mult) \
                    .then_inc(sig("pick_ready"), 1)
                wait(dve, "pick_ready", b + 1)
                for t in range(NT):
                    for h in range(2):
                        wait(dve, "experts_done", 2 * NT * b + 2 * t + h + 1)
                        wait(dve, "summed", NT * b + t - 1 if t >= 2 else NT * b)
                        nc.vector.tensor_tensor(
                            ebuf[:, t % 2, 4 * h:4 * h + 4, :],
                            psM[:, h * HALF:(h + 1) * HALF].rearrange("p (e d) -> p e d", d=D),
                            pick[:, t, 4 * h:4 * h + 4].unsqueeze(2).broadcast_to([P, 4, D]), ALU.mult) \
                            .then_inc(sig("picked"), 1)
                wait(dve, "pickT_done", b + 1)
                nc.vector.tensor_copy(pickT[:, :], psY[0:NT * E, 0:P]).then_inc(sig("pickT_ready"), 1)
                wait(dve, "ebias_done", b + 1)
                wait(dve, "summed", NT * (b + 1))
                nc.vector.tensor_tensor(xb(gate, b), xb(gate, b), psH[:, :, :].rearrange("p a b -> p (a b)"),
                                        ALU.add).then_inc(sig("z_ready"), 1)

            batches(dve, expert_batch)

            def add_y(f, batch, half):
                wait(dve, "y_done", 2 * f + half + 1)
                nc.vector.tensor_tensor(xb(X, batch, half * HALF, HALF), xb(X, batch, half * HALF, HALF), psY[:, :],
                                        ALU.add).then_inc(sig("y_added"), 1)

            def norm1_statistics(m, batch, par):
                wait(dve, "y_added", 2 * (m - 4) + 2)
                wait(dve, "xh1_ready", NT * (m - 1))
                tile_statistics(lambda t: xb(X, batch, t * P, P), "n1")
                token_statistics(0, par, "n1", m + 1)

            def slot(l, j):
                (attn, _), (norm2, _), (ffn, lf) = items(l, j)
                n = 4 * l + j
                f = n - 2
                par = j % 2
                fbatch = (j - 2) % 4
                nbatch = (j - 1) % 4

                def leaky(i):
                    if ffn:
                        wait(dve, "hsl_ready", NF * f + i + 1)
                        nc.vector.tensor_tensor(hid[:, i % NC, :], psH[:, i % 2, :], hsl[:, i % 2, :], ALU.max) \
                            .then_inc(sig("hid_ready"), 1)

                if attn and j == 0:
                    wait(dve, "k_done", n)
                    wait(dve, "ctx_done", n)
                    wait(dve, "xnT_ready", n)
                    nc.vector.tensor_copy(lns[:, 0:1], param(0, l))
                    nc.vector.tensor_copy(lns[:, 1:2], param(1, l))
                    nc.vector.tensor_copy(wk_s[:, :], of_layer(wk_all, l, 0, D))
                    nc.vector.tensor_copy(wv_s[:, :], of_layer(wv_all, l, 0, D)).then_inc(sig("wkv_staged"), 1)
                if attn and j == 1:
                    wait(dve, "xn2_ready", n - 1)
                    nc.vector.tensor_copy(lns[:, 2:3], param(2, l))
                    nc.vector.tensor_copy(lns[:, 3:4], param(3, l)).then_inc(sig("ln2_staged"), 1)
                if ffn:
                    wait(dve, "xn2_ready", f + 1)
                    wait(dve, "h_done", NF * f)
                    nc.vector.tensor_copy(xn2_hi[:, :], xn2[:, :]).then_inc(sig("xn2_hi_ready"), 1)
                if norm2:
                    wait(dve, "attn_done", n)
                    nc.vector.tensor_tensor(xb(X, nbatch), xb(X, nbatch), psM[:, :], ALU.add) \
                        .then_inc(sig("x1_added"), 1)
                last_ffn = 4 * l + j - 3
                if not isinstance(last_ffn, int) or last_ffn >= 0:
                    add_y(last_ffn, (j - 3) % 4, 1)
                if norm2:
                    wait(dve, "x1_added", n)
                    wait(dve, "shift2_ready", n - 1)
                    tile_statistics(lambda t: xb(X, nbatch, t * P, P), "n2")
                leaky(0)
                leaky(1)
                if attn:
                    wait(dve, "k_done", n + 1)
                    nc.vector.tensor_reduce(negkmax[:, par:par + 1], psT[:, :], AX_X, ALU.max, negate=True) \
                        .then_inc(sig("negkmax_ready"), 1)
                if norm2:
                    token_statistics(1, 0, "n2", n)
                if attn:
                    wait(dve, "q_done", n + 1)
                    nc.vector.tensor_reduce(qmax[:, :], by_head(psM[:, :]), AX_X, ALU.max) \
                        .then_inc(sig("qmax_ready"), 1)
                leaky(2)
                if attn:
                    if j == 0:
                        wait(dve, "bv_done", l + 1)
                        nc.vector.tensor_scalar(bvm[:, :], ones[:, :], psS[:, 0:1], 1.0 / H, ALU.mult, ALU.mult) \
                            .then_inc(sig("bv_ready"), 1)
                    wait(dve, "qmax_ready", n + 1)
                    wait(dve, "qsm_ready", n)
                    nc.vector.tensor_tensor(by_head(qe[:, :]), by_head(psM[:, :]), over_head(qmax[:, :]),
                                            ALU.subtract).then_inc(sig("qe_ready"), 1)
                    if j == 0:
                        wait(dve, "bias_done", l + 1)
                        nc.vector.tensor_copy(bias_row[:, :], psS[:, 0:D]).then_inc(sig("bias_ready"), 1)
                leaky(3)
                if attn:
                    wait(dve, "expq_ready", n + 1)
                    nc.vector.tensor_reduce(qsum[:, :], by_head(qe[:, :]), AX_X, ALU.add) \
                        .then_inc(sig("qsum_ready"), 1)
                leaky(4)
                if attn:
                    wait(dve, "qsum_ready", n + 1)
                    nc.vector.reciprocal(qrec[:, :], qsum[:, :]).then_inc(sig("qrec_ready"), 1)
                    nc.vector.reciprocal(krec[:, :], ksum[:, par:par + 1]).then_inc(sig("krec_ready"), 1)
                    wait(dve, "g_done", n + 1)
                    nc.vector.tensor_scalar(gT[:, :], psS[:, 0:D], lns[:, 0:1], None, ALU.mult) \
                        .then_inc(sig("gT_ready"), 1)
                leaky(5)
                if ffn:
                    add_y(f, fbatch, 0)
                if attn:
                    wait(dve, "ctx_done", n + 1)
                    nc.vector.tensor_tensor(ctxT[:, :], psS[:, 0:D], head_mask[:, :], ALU.mult) \
                        .then_inc(sig("ctx_ready"), 1)
                nxt = n + 1
                if not (isinstance(nxt, int) and nxt >= 4 * L):
                    norm1_statistics(nxt, (j + 1) % 4, (j + 1) % 2)
                leaky(6)
                if attn:
                    wait(dve, "mix_done", n + 1)
                    wait(dve, "krec_ready", n + 1)
                    nc.vector.scalar_tensor_tensor(mix[:, :], psS[:, 0:D], krec[:, 0:1], bias_row[:, :],
                                                   ALU.mult, ALU.add).then_inc(sig("mix_ready"), 1)
                leaky(7)
                if j == 1:
                    if attn:
                        wait(dve, "h_done", NF * (4 * l))
                        nc.vector.tensor_copy(w1_hi[:, :, :],
                                              of_layer(w1_all, l, 0, FF).rearrange("p (m c) -> p c m", c=NC)) \
                            .then_inc(sig("w1_hi_ready"), 1)

            wait(dve, "param_loaded", 16 * 2)
            wait(dve, "attn_loaded", 16 * 4 * L)
            wait(dve, "ffn_loaded", 16 * 2 * L)
            wait(dve, "x0_ready", NBATCH)
            norm1_statistics(0, 0, 0)
            slots(dve, slot)
            add_y(4 * L - 1, 3, 1)
            wait(dve, "gate_ready", NBATCH)
            for b in range(NBATCH):
                if b == NBATCH - 1:
                    wait(dve, "y_added", 2 * 4 * L)
                nc.vector.tensor_tensor(gate[:, b, :], gate[:, b, :], X[:, b, :], ALU.mult) \
                    .then_inc(sig("gated"), 1)

        @block.gpsimd
        def _(pool):
            nc.gpsimd.memset(ident[:, :], 0.0).then_inc(sig("const_ready"), 1)
            nc.gpsimd.memset(head_mask[:, :], 1.0).then_inc(sig("const_ready"), 1)
            nc.gpsimd.memset(minus_half[:, :], -0.5).then_inc(sig("const_ready"), 1)
            nc.gpsimd.memset(eb_diag[:, :, :], 0.0).then_inc(sig("const_ready"), 1)
            pool.wait_ge(sig("const_ready"), 4)
            nc.gpsimd.affine_select(out=ident[:, :], in_=ident[:, :], compare_op=ALU.not_equal, fill=1.0, base=0,
                                    pattern=[[-1, P]], channel_multiplier=1).then_inc(sig("const_ready"), 1)
            for t in range(NT):
                pool.dma_start(eb_diag[E * t:E * (t + 1), t, :], expert_b).then_inc(sig("eb_loaded"), 16)
            by = head_mask[:, :].rearrange("p (g d) -> p g d", d=DH)
            nc.gpsimd.affine_select(out=by, in_=by, compare_op=ALU.is_ge, fill=0.0, base=0,
                                    pattern=[[-DH, H], [0, DH]], channel_multiplier=1) \
                .then_inc(sig("mask_step"), 1)
            pool.wait_ge(sig("mask_step"), 1)
            nc.gpsimd.affine_select(out=by, in_=by, compare_op=ALU.is_ge, fill=0.0, base=DH - 1,
                                    pattern=[[DH, H], [0, DH]], channel_multiplier=-1) \
                .then_inc(sig("mask_ready"), 1)
            for e in range(E):
                nc.gpsimd.memset(rank[:, e:e + 1], float(E - e)).then_inc(sig("rank_ready"), 1)

            def expert_batch(b):
                wait(pool, "n0_var", b + 1)
                nc.gpsimd.tensor_tensor(rstd[:, 0, 0, :], veps[:, 0, 0, :], minus_half[:, :], ALU.pow) \
                    .then_inc(sig("n0_rstd"), 1)
                wait(pool, "xn0_hi_ready", b + 1)
                nc.gpsimd.tensor_tensor(xn2_lo[:, :], xnT[:, :], xn2_hi[:, :].bitcast(F32), ALU.subtract) \
                    .then_inc(sig("xn0_split"), 1)
                for t in range(NT):
                    wait(pool, "picked", 2 * NT * b + 2 * t + 2)
                    a = ebuf[:, t % 2, :, :]
                    nc.gpsimd.tensor_tensor(a[:, 0:4, :], a[:, 0:4, :], a[:, 4:8, :], ALU.add) \
                        .then_inc(sig("sum4"), 1)
                    wait(pool, "sum4", NT * b + t + 1)
                    nc.gpsimd.tensor_tensor(a[:, 0:2, :], a[:, 0:2, :], a[:, 2:4, :], ALU.add) \
                        .then_inc(sig("sum2"), 1)
                    wait(pool, "sum2", NT * b + t + 1)
                    nc.gpsimd.tensor_tensor(xb(gate, b, t * P, P), a[:, 0, :], a[:, 1, :], ALU.add) \
                        .then_inc(sig("summed"), 1)

            batches(pool, expert_batch)

            def norm1(m, batch, par):
                wait(pool, "n1_var", m + 1)
                nc.gpsimd.tensor_tensor(rstd[:, 0, par, :], veps[:, 0, par, :], minus_half[:, :], ALU.pow) \
                    .then_inc(sig("n1_rstd"), 1)
                pool.wait_ge(sig("const_ready"), 5)
                wait(pool, "n1_rstd", m + 1)
                wait(pool, "g_done", m - 1)
                for t in range(NT):
                    nc.gpsimd.tensor_scalar(tile(xh1[:, par, :], t), xb(X, batch, t * P, P),
                                            mean[:, 0, par, t:t + 1], rstd[:, 0, par, t:t + 1],
                                            ALU.subtract, ALU.mult).then_inc(sig("xh1_ready"), 1)

            def slot(l, j):
                (attn, _), (norm2, _), (ffn, _) = items(l, j)
                n = 4 * l + j
                f = n - 2
                if ffn:
                    wait(pool, "xn2_hi_ready", f + 1)
                    nc.gpsimd.tensor_tensor(xn2_lo[:, :], xn2[:, :], xn2_hi[:, :].bitcast(F32), ALU.subtract) \
                        .then_inc(sig("xn2_lo_ready"), 1)
                if norm2:
                    wait(pool, "n2_var", n)
                    wait(pool, "xh2_ready", NT * (n - 1))
                    nc.gpsimd.tensor_tensor(rstd[:, 1, 0, :], veps[:, 1, 0, :], minus_half[:, :], ALU.pow) \
                        .then_inc(sig("n2_rstd"), 1)
                    wait(pool, "n2_rstd", n)
                    nc.gpsimd.tensor_tensor(shift2[:, :], mean[:, 1, 0, :], rstd[:, 1, 0, :], ALU.mult) \
                        .then_inc(sig("shift2_ready"), 1)
                if attn:
                    wait(pool, "qrec_ready", n + 1)
                    wait(pool, "tq_done", n)
                    nc.gpsimd.tensor_tensor(by_head(qsm[:, :]), by_head(qe[:, :]), over_head(qrec[:, :]), ALU.mult) \
                        .then_inc(sig("qsm_ready"), 1)
                if not (isinstance(n, int) and n + 1 >= 4 * L):
                    norm1(n + 1, (j + 1) % 4, (j + 1) % 2)
                if attn and j == 1:
                    wait(pool, "w1_hi_ready", l + 1)
                    nc.gpsimd.tensor_tensor(w1_lo[:, :, :],
                                            of_layer(w1_all, l, 0, FF).rearrange("p (m c) -> p c m", c=NC),
                                            w1_hi[:, :, :].bitcast(F32), ALU.subtract).then_inc(sig("w1_staged"), 1)

            norm1(0, 0, 0)
            slots(pool, slot)
            for b in range(NBATCH):
                wait(pool, "gated", b + 1)
                nc.gpsimd.tensor_tensor(xraw[:, b, :], xraw[:, b, :], gate[:, b, :], ALU.add) \
                    .then_inc(sig("out_ready"), 1)


_OUTS = [((4, 1024, 128), 'float32')]


def kernel(**inputs):
    import numpy as _np
    import concourse.bacc as _bacc
    from concourse import mybir as _mybir
    from concourse.bass_utils import run_bass_kernel_spmd as _run

    a = {k[3:]: _np.asarray(v) for k, v in inputs.items()}
    laid_out = {
        "x": a["attn_x"],
        "ln_params": _np.stack([a[f"attn_{k}"].T for k in ("ln1_w", "ln1_b", "ln2_w", "ln2_b")], axis=1),
        "wq": a["attn_wq"], "wk": a["attn_wk"], "wv": a["attn_wv"], "wo": a["attn_wo"], "bo": a["attn_bo"],
        "w1": a["attn_w1"], "w2": a["attn_w2"],
        "router_wT": a["ffn_router_w"].T, "router_b": a["ffn_router_b"],
        "expert_wT": a["ffn_expert_w"].transpose(2, 0, 1), "expert_b": a["ffn_expert_b"],
    }
    nc = _bacc.Bacc("TRN2", target_bir_lowering=False, num_devices=1)
    arrays, args = {}, []
    for name, value in laid_out.items():
        value = _np.ascontiguousarray(value)
        arrays[f"in_{name}_dram"] = value
        args.append(nc.dram_tensor(f"in_{name}_dram", value.shape, _mybir.dt.from_np(value.dtype),
                                   kind="ExternalInput").ap())
    for i, (shape, dtype) in enumerate(_OUTS):
        dt = _mybir.dt.from_np(_np.dtype(dtype))
        args.append(nc.dram_tensor(f"out_{i}_dram", shape, dt, kind="ExternalOutput").ap())
    build_program(nc, *args)
    r = _run(nc, [arrays], core_ids=[0])
    return r.results[0]["out_0_dram"]
```

```python
from contextlib import ExitStack

import concourse.bass as bass
from concourse import mybir

ALU = mybir.AluOpType
ACT = mybir.ActivationFunctionType
AX_X = mybir.AxisListType.X
F32 = mybir.dt.float32
F32R = mybir.dt.float32r
I32 = mybir.dt.int32

EPS = 1e-5
SLOPE = 0.01


def build_program(nc, x_in, ln_params, wq, wk, wv, wo, bo, w1, w2, router_wT, router_b, expert_wT, expert_b, out):
    NBATCH, T, D = x_in.shape
    L = wq.shape[0]
    FF = w1.shape[2]
    E = router_wT.shape[1]
    H = 8
    DH = D // H
    P = 128
    NT = T // P
    HALF = T // 2
    NC = FF // P
    NF = 2 * NC
    assert NBATCH == 4 and D == P and NT == 8 and NC == 4 and E == 8

    with ExitStack() as ctx:
        def sb(name, shape, dt=F32):
            return ctx.enter_context(nc.sbuf_tensor(name, shape, dt))

        def ps(name, shape):
            return ctx.enter_context(nc.psum_tensor(name, shape, F32))

        def sem(name):
            return ctx.enter_context(nc.semaphore(name))

        psT = ps("psT", [P, T])
        psM = ps("psM", [P, T])
        psY = ps("psY", [P, HALF])
        psS = ps("psS", [P, HALF])
        psH = ps("psH", [P, 2, HALF])

        tokens = sb("tokens", [P, 2 * NBATCH, T])
        xraw = tokens[:, 0:NBATCH, :]
        X = tokens[:, NBATCH:, :]
        gate = sb("gate", [P, NBATCH, T])
        wq_all = sb("wq_all", [P, L, D])
        wk_all = sb("wk_all", [P, L, D])
        wv_all = sb("wv_all", [P, L, D])
        wo_all = sb("wo_all", [P, L, D])
        w1_all = sb("w1_all", [P, L, FF])
        w2_all = sb("w2_all", [P, L, NC, D])
        lnp = sb("lnp", [P, 4, L])
        lns = sb("lns", [P, 4])
        bo_row = sb("bo_row", [1, L, D])
        wk_s = sb("wk_s", [P, D])
        wv_s = sb("wv_s", [P, D])
        w1_hi = sb("w1_hi", [P, NC, P], F32R)
        w1_lo = sb("w1_lo", [P, NC, P], F32R)
        ident = sb("ident", [P, P])
        head_mask = sb("head_mask", [P, P])
        ones = sb("ones", [P, P])
        eighth = sb("eighth", [1, P])
        minus_half = sb("minus_half", [P, NT])
        rank = sb("rank", [P, E])
        st = sb("st", [P, 2, NT, 6])
        sdiff = sb("sdiff", [P, 2, NT])
        sdev = sb("sdev", [P, 2, NT])
        negmean = sb("negmean", [P, 2, NT])
        veps = sb("veps", [P, 2, NT])
        rstd = sb("rstd", [P, 2, NT])
        shift = sb("shift", [P, 2, NT])
        xh1 = sb("xh1", [P, 2, T])
        xnT = sb("xnT", [P, T])
        negkmax = sb("negkmax", [P, 2])
        ksum = sb("ksum", [P, 2])
        krec = sb("krec", [P, 1])
        expk = sb("expk", [P, T])
        expkT = sb("expkT", [P, T])
        qmax = sb("qmax", [P, NT * H])
        qsum = sb("qsum", [P, NT * H])
        qrec = sb("qrec", [P, NT * H])
        qe = sb("qe", [P, T])
        qsm = sb("qsm", [P, T])
        qsmT = sb("qsmT", [P, T])
        gT = sb("gT", [P, D])
        ctxT = sb("ctxT", [P, D])
        mix = sb("mix", [P, D])
        bvm = sb("bvm", [P, D])
        bias_row = sb("bias_row", [P, D])
        xh2 = sb("xh2", [P, T])
        xn2 = sb("xn2", [P, T])
        xn2_hi = sb("xn2_hi", [P, T], F32R)
        xn2_lo = sb("xn2_lo", [P, T], F32R)
        hsl = sb("hsl", [P, 2, HALF])
        hid = sb("hid", [P, NC, HALF])
        ewn = sb("ewn", [P, E, D])
        ew_hi = sb("ew_hi", [P, E, D], F32R)
        ew_lo = sb("ew_lo", [P, E, D], F32R)
        rwT = sb("rwT", [P, E])
        rb_bc = sb("rb_bc", [P, E])
        eb_diag = sb("eb_diag", [NT * E, NT, D])
        lg = sb("lg", [P, NT, E])
        lmax = sb("lmax", [P, NT])
        eq = sb("eq", [P, NT, E])
        lmax2 = sb("lmax2", [P, NT])
        pick = sb("pick", [P, NT, E])
        le = sb("le", [P, NT, E])
        lsum = sb("lsum", [P, NT])
        lrec = sb("lrec", [P, NT])
        pickT = sb("pickT", [NT * E, P])
        NBUF = 4
        ebuf = sb("ebuf", [P, NBUF, E, D])

        ACT_PRODUCT = (0, 1, 2, 3, 4, 5, 6, 7)
        DVE_SUM = (3, 7)

        def act_products(t):
            return sum(u < t for u in ACT_PRODUCT)

        def dve_products(t):
            return 2 * t - act_products(t)

        def dve_sums(t):
            return sum(u < t for u in DVE_SUM)

        def pool_sums(t):
            return t - dve_sums(t)

        def through(upto, b, t):
            return upto(NT) * b + upto(t + 1) if t >= 0 else upto(NT) * (b - 1) + upto(NT + t + 1)

        S = {}

        def sig(name):
            if name not in S:
                S[name] = sem(name)
            return S[name]

        def wait(eng, name, value):
            if isinstance(value, int) and value <= 0:
                return
            eng.wait_ge(sig(name), value)

        def tile(a, t):
            return a[:, t * P:(t + 1) * P]

        def by_head(a):
            return a.rearrange("p (g d) -> p g d", d=DH)

        def over_head(a):
            return a.unsqueeze(2).broadcast_to([P, NT * H, DH])

        def xb(a, b, lo=0, n=T):
            if isinstance(b, int):
                return a[:, b, lo:lo + n]
            return a[:, :, :].rearrange("p b t -> p (b t)")[:, bass.ds(b * T + lo, n)]

        def of_layer(a, l, lo, n):
            flat = a[:, :, :, :].rearrange("p l c d -> p (l c d)") if len(a.shape) == 4 \
                else a[:, :, :].rearrange("p l d -> p (l d)")
            w = flat.shape[1] // L
            if isinstance(l, int):
                return flat[:, l * w + lo:l * w + lo + n]
            return flat[:, bass.ds(l * w + lo, n)]

        def param(k, l):
            if isinstance(l, int):
                return lnp[:, k, l:l + 1]
            return lnp[:, k, bass.ds(l, 1)]

        def batches(eng, body):
            body(0, True)
            with eng.Fori(1, NBATCH - 1) as b:
                body(b, True)
            body(NBATCH - 1, False)

        def slots(eng, slot):
            for j in range(4):
                slot(0, j)
            with eng.Fori(1, L) as l:
                for j in range(4):
                    slot(l, j)
            for j in range(2):
                slot(L, j)

        def items(l, j):
            def there(lag):
                if isinstance(l, int):
                    n = 4 * l + j - lag
                    return 0 <= n < 4 * L
                return True
            return (there(0), l), (there(1), l if j >= 1 else l - 1), (there(2), l if j >= 2 else l - 1)

        def norm1_next(l, j):
            n = 4 * l + j
            return not isinstance(n, int) or n + 1 < 4 * L

        block = ctx.enter_context(nc.Block())

        @block.sync
        def _(sp):
            sp.dma_start(xraw[:, 0, :], x_in[0].rearrange("(p t) d -> p (t d)", p=P)) \
                .then_inc(sig("x_first_loaded"), 16)
            sp.dma_start(ewn[:, :, :], expert_wT).then_inc(sig("expert_loaded"), 16)
            for b in range(1, NBATCH):
                sp.dma_start(xraw[:, b, :], x_in[b].rearrange("(p t) d -> p (t d)", p=P)) \
                    .then_inc(sig("x_loaded"), 16)
            for l in range(L):
                sp.dma_start(wk_all[:, l, :], wk[l]).then_inc(sig("attn_loaded"), 16)
                sp.dma_start(wq_all[:, l, :], wq[l]).then_inc(sig("attn_loaded"), 16)
                sp.dma_start(wv_all[:, l, :], wv[l]).then_inc(sig("attn_loaded"), 16)
                sp.dma_start(wo_all[:, l, :], wo[l]).then_inc(sig("attn_loaded"), 16)
                sp.dma_start(w1_all[:, l, :], w1[l]).then_inc(sig("ffn_loaded"), 16)
                sp.dma_start(w2_all[:, l, :, :], w2[l].rearrange("(p c) d -> p c d", c=NC)) \
                    .then_inc(sig("ffn_loaded"), 16)
            for b in range(NBATCH):
                sp.wait_ge(sig("out_ready"), b + 1)
                sp.dma_start(out[b].rearrange("(p t) d -> p (t d)", p=P), xraw[:, b, :]) \
                    .then_inc(sig("stored"), 16)
            sp.wait_ge(sig("stored"), 16 * NBATCH)

        @block.tensor
        def _(pe):
            def transposes(dst, src):
                for t in range(NT):
                    last = nc.tensor.transpose(tile(dst, t), tile(src, t), ident[:, :])
                return last

            def split_product(dst, hi_w, lo_w, hi_x, lo_x):
                nc.tensor.matmul(dst, hi_w, hi_x, start=True, stop=False)
                nc.tensor.matmul(dst, lo_w, hi_x, start=False, stop=False)
                return nc.tensor.matmul(dst, hi_w, lo_x, start=False, stop=True)

            def normalised_tiles(b):
                pe.wait_ge(sig("const_ready"), 5)
                pe.wait_ge(sig("xh0_ready"), b + 1)
                transposes(psT, xh1[:, 0, :]).then_inc(sig("t0_done"), 1)

            def logits(b):
                pe.wait_ge(sig("router_loaded"), 32)
                pe.wait_ge(sig("xn0T_ready"), b + 1)
                for t in range(NT):
                    last = nc.tensor.matmul(psS[:, t * E:(t + 1) * E], tile(xnT, t), rwT[:, :],
                                            start=True, stop=True)
                last.then_inc(sig("logits_done"), 1)

            def picked_bias(b, half):
                pe.wait_ge(sig("pickT_ready"), b + 1)
                wait(pe, "bias_added", 2 * b + half)
                for t in range(4):
                    last = nc.tensor.matmul(tile(psY, t), pickT[:, :], eb_diag[:, 4 * half + t, :],
                                            start=True, stop=True)
                last.then_inc(sig("ebias_done"), 1)

            def expert_batch(b, more):
                for t in range(NT):
                    if t % 4 == 0:
                        pe.wait_ge(sig("xn0_lo_ready"), 2 * b + t // 4 + 1)
                    bank = (psM[:, :], psH[:, :, :].rearrange("p a b -> p (a b)"))[t % 2]
                    wait(pe, "picked_dve", through(dve_products, b, t - 2))
                    wait(pe, "picked_act", through(act_products, b, t - 2))
                    for h in range(2):
                        split_product(bank[:, h * HALF:(h + 1) * HALF], tile(xn2_hi, t), tile(xn2_lo, t),
                                      ew_hi[:, 4 * h:4 * h + 4, :], ew_lo[:, 4 * h:4 * h + 4, :]) \
                            .then_inc(sig("experts_done"), 1)
                    if t in (1, 3) and not (isinstance(b, int) and b == 0):
                        picked_bias(b - 1, t // 2)
                    if t == 3 and more:
                        normalised_tiles(b + 1)
                    if t == 5 and more:
                        logits(b + 1)
                    if t == 5:
                        pe.wait_ge(sig("const_ready"), 5)
                        wait(pe, "bias_added", 2 * b)
                        nc.tensor.transpose(psY[0:NT * E, 0:P], pick[:, :, :].rearrange("p t e -> p (t e)"),
                                            ident[:, :]).then_inc(sig("pickT_done"), 1)

            normalised_tiles(0)
            logits(0)
            pe.wait_ge(sig("ew_split"), 1)
            pe.wait_ge(sig("eb_loaded"), 16 * NT)
            batches(pe, expert_batch)
            for half in range(2):
                picked_bias(NBATCH - 1, half)

            def w1_step(f, i):
                half, c = i // NC, i % NC
                if c == 0:
                    pe.wait_ge(sig("xn2_lo_ready"), 2 * f + half + 1)
                wait(pe, "hid_ready", NF * f + i - 1)
                cols = slice(half * HALF, (half + 1) * HALF)
                split_product(psH[:, i % 2, :], w1_hi[:, c, :], w1_lo[:, c, :], xn2_hi[:, cols], xn2_lo[:, cols]) \
                    .then_inc(sig("h_done"), 1)

            def w2_step(f, l, i):
                c = i % NC
                pe.wait_ge(sig("hid_ready"), NF * f + i + 1)
                if c == 0:
                    wait(pe, "y_added", 2 * f + i // NC)
                for t in range(4):
                    last = nc.tensor.matmul(tile(psY, t), tile(hid[:, i % NC, :], t), of_layer(w2_all, l, c * D, D),
                                            start=(c == 0 and t == 0), stop=(c == NC - 1), skip_group_check=True)
                if c == NC - 1:
                    last.then_inc(sig("y_done"), 1)

            def slot(l, j):
                (attn, _), (norm2, _), (ffn, lf) = items(l, j)
                n = 4 * l + j
                f = n - 2

                def ffn_step(i):
                    if ffn:
                        if i < NF:
                            if i == 0 and j == 2:
                                pe.wait_ge(sig("w1_staged"), l + 1)
                            w1_step(f, i)
                        if i >= 2:
                            w2_step(f, lf, i - 2)

                ffn_step(0)
                ffn_step(1)
                if attn:
                    pe.wait_ge(sig("xnT_ready"), n + 1)
                    if j == 0:
                        pe.wait_ge(sig("wkv_staged"), l + 1)
                    for h in (0, 1):
                        last = nc.tensor.matmul(psT[:, h * HALF:(h + 1) * HALF], wk_s[:, :],
                                                xnT[:, h * HALF:(h + 1) * HALF], start=True, stop=True)
                    last.then_inc(sig("k_done"), 1)
                    wait(pe, "x1_added", n)
                    for t in range(NT):
                        last = nc.tensor.matmul(tile(psM, t), tile(xnT, t), of_layer(wq_all, l, 0, D),
                                                start=True, stop=True)
                    last.then_inc(sig("q_done"), 1)
                    if j == 0:
                        wait(pe, "mix_ready", n)
                        nc.tensor.matmul(psS[:, 0:1], wv_s[:, :], lns[:, 1:2], start=True, stop=True) \
                            .then_inc(sig("bv_done"), 1)
                ffn_step(2)
                if attn:
                    pe.wait_ge(sig("expk_ready"), n + 1)
                    transposes(psT, expk).then_inc(sig("tk_done"), 1)
                    if j == 0:
                        pe.wait_ge(sig("bv_ready"), l + 1)
                        nc.tensor.matmul(psS[:, 0:D], bvm[:, :], of_layer(wo_all, l, 0, D), start=True, stop=False)
                        nc.tensor.matmul(psS[:, 0:D], eighth[:, :], of_layer(bo_row, l, 0, D),
                                         start=False, stop=True).then_inc(sig("bias_done"), 1)
                ffn_step(3)
                ffn_step(4)
                if attn:
                    pe.wait_ge(sig("expkT_ready"), n + 1)
                    wait(pe, "mix_ready", n)
                    pe.wait_ge(sig("bias_ready"), l + 1)
                    for t in range(NT):
                        last = nc.tensor.matmul(psS[:, 0:D], tile(xh1[:, j % 2, :], t), tile(expkT, t),
                                                start=(t == 0), stop=(t == NT - 1))
                    last.then_inc(sig("g_done"), 1)
                ffn_step(5)
                if attn:
                    pe.wait_ge(sig("gT_ready"), n + 1)
                    nc.tensor.matmul(psS[:, 0:D], wv_s[:, :], gT[:, :], start=True, stop=True) \
                        .then_inc(sig("ctx_done"), 1)
                ffn_step(6)
                if attn:
                    pe.wait_ge(sig("ctx_ready"), n + 1)
                    nc.tensor.matmul(psS[:, 0:D], ctxT[:, :], of_layer(wo_all, l, 0, D), start=True, stop=True) \
                        .then_inc(sig("mix_done"), 1)
                    pe.wait_ge(sig("qsm_ready"), n + 1)
                    transposes(psT, qsm).then_inc(sig("tq_done"), 1)
                ffn_step(7)
                if norm2:
                    wait(pe, "xh2_ready", NT * n)
                    if attn:
                        pe.wait_ge(sig("qsmT_ready"), n + 1)
                    transposes(psT, xh2).then_inc(sig("t2_done"), 1)
                if attn:
                    pe.wait_ge(sig("mix_ready"), n + 1)
                    pe.wait_ge(sig("qsmT_ready"), n + 1)
                    pe.wait_ge(sig("qe_ready"), n + 1)
                    for t in range(NT):
                        last = nc.tensor.matmul(tile(psM, t), tile(qsmT, t), mix[:, :], start=True, stop=True)
                    last.then_inc(sig("attn_done"), 1)
                ffn_step(8)
                if norm1_next(l, j):
                    pe.wait_ge(sig("xh1a_ready"), 4 * (n + 2))
                    pe.wait_ge(sig("xh1b_ready"), n + 2)
                    pe.wait_ge(sig("qsmT_ready"), n + 1)
                    wait(pe, "xn2_ready", n)
                    transposes(psT, xh1[:, (j + 1) % 2, :]).then_inc(sig("t1_done"), 1)
                ffn_step(9)

            pe.wait_ge(sig("ffn_loaded"), 16 * 2 * L)
            pe.wait_ge(sig("attn_loaded"), 16 * 4 * L)
            pe.wait_ge(sig("param_loaded"), 16 * 2)
            pe.wait_ge(sig("ones_ready"), 1)
            pe.wait_ge(sig("picked_dve"), NBATCH * dve_products(NT))
            pe.wait_ge(sig("picked_act"), NBATCH * act_products(NT))
            pe.wait_ge(sig("bias_added"), 2 * NBATCH)
            pe.wait_ge(sig("xh1a_ready"), 4)
            pe.wait_ge(sig("xh1b_ready"), 1)
            transposes(psT, xh1[:, 0, :]).then_inc(sig("t1_done"), 1)
            slots(pe, slot)

        @block.scalar
        def _(act):
            act.dma_start(rwT[:, :], router_wT).then_inc(sig("router_loaded"), 16)
            act.dma_start(rb_bc[:, :], router_b.rearrange("(a e) -> a e", a=1).broadcast_to([P, E])) \
                .then_inc(sig("router_loaded"), 16)
            act.dma_start(lnp[:, :, :], ln_params).then_inc(sig("param_loaded"), 16)
            act.dma_start(bo_row[:, :, :], bo.rearrange("l (a d) -> a l d", a=1)).then_inc(sig("param_loaded"), 16)

            def normalise_input(b, tiles):
                if tiles.start == 0:
                    act.wait_ge(sig("ln1_shift"), b + 1)
                    wait(act, "t0_done", b)
                    wait(act, "x0_ready", b)
                for t in tiles:
                    last = nc.scalar.activation(tile(xh1[:, 0, :], t), xb(xraw, b, t * P, P), ACT.Identity,
                                                bias=shift[:, 0, t:t + 1], scale=rstd[:, 0, t:t + 1])
                if tiles.stop == NT:
                    last.then_inc(sig("xh0_ready"), 1)

            def residual_stream(b):
                act.wait_ge(sig("xh0_ready"), b + 1)
                nc.scalar.activation(xb(X, b), xh1[:, 0, :], ACT.Copy).then_inc(sig("x0_ready"), 1)

            def feature_major(b):
                act.wait_ge(sig("t0_done"), b + 1)
                wait(act, "xn0_lo_ready", 2 * b)
                nc.scalar.activation(xnT[:, :], psT[:, :], ACT.Copy).then_inc(sig("xn0T_ready"), 1)

            def router_exponentials(b):
                act.wait_ge(sig("lsub_ready"), b + 1)
                nc.scalar.activation(le[:, :, :], lg[:, :, :], ACT.Exp).then_inc(sig("lexp_ready"), 1)

            def expert_batch(b, more):
                for t in range(NT):
                    if t in ACT_PRODUCT:
                        act.wait_ge(sig("experts_done"), 2 * NT * b + 2 * t + 2)
                        act.wait_ge(sig("pick_ready"), b + 1)
                        wait(act, "dve_summed", through(dve_sums, b, t - NBUF))
                        wait(act, "pool_summed", through(pool_sums, b, t - NBUF))
                        bank = (psM[:, HALF:], psH[:, 1, :])[t % 2]
                        for e in range(4):
                            last = nc.scalar.activation(ebuf[:, t % NBUF, 4 + e, :], tile(bank, e), ACT.Copy,
                                                        scale=pick[:, t, 4 + e:5 + e])
                        last.then_inc(sig("picked_act"), 1)
                    if more and t < 3:
                        normalise_input(b + 1, range(3 * t, min(3 * t + 3, NT)))
                    if more and t == 4:
                        feature_major(b + 1)
                        residual_stream(b + 1)
                    if more and t == 6:
                        router_exponentials(b + 1)

            normalise_input(0, range(NT))
            act.wait_ge(sig("expert_loaded"), 16)
            nc.scalar.activation(ew_hi[:, :, :], ewn[:, :, :], ACT.Copy) \
                .then_inc(sig("ew_hi_ready"), 1)
            feature_major(0)
            residual_stream(0)
            router_exponentials(0)
            batches(act, expert_batch)

            def gates():
                act.wait_ge(sig("bias_added"), 2 * NBATCH)
                for b in range(NBATCH):
                    last = nc.scalar.activation(gate[:, b, :], gate[:, b, :], ACT.Silu)
                last.then_inc(sig("gate_ready"), 1)

            def slot(l, j):
                (attn, _), (norm2, lm), (ffn, _) = items(l, j)
                n = 4 * l + j
                f = n - 2

                def slope(i):
                    if ffn:
                        act.wait_ge(sig("h_done"), NF * f + i + 1)
                        nc.scalar.activation(hsl[:, i % 2, :], psH[:, i % 2, :], ACT.Copy, scale=SLOPE) \
                            .then_inc(sig("hsl_ready"), 1)

                def normalise(norm, tiles):
                    if not (norm2, norm1_next(l, j))[norm == 0]:
                        return
                    if tiles.start == 0 and norm == 0:
                        act.wait_ge(sig("ln1_shift"), NBATCH + n + 2)
                        wait(act, "g_done", n)
                    elif tiles.start == 0:
                        wait(act, "ln2_shift", n)
                        wait(act, "t2_done", n - 1)
                    dst = xh1[:, (j + 1) % 2, :] if norm == 0 else xh2
                    batch = (j + 1) % 4 if norm == 0 else (j - 1) % 4
                    for t in tiles:
                        nc.scalar.activation(tile(dst, t), xb(X, batch, t * P, P), ACT.Identity,
                                             bias=shift[:, norm, t:t + 1], scale=rstd[:, norm, t:t + 1]) \
                            .then_inc(sig(("xh1a_ready", "xh2_ready")[norm]), 1)

                if attn:
                    act.wait_ge(sig("t1_done"), n + 1)
                    wait(act, "q_done", n)
                    if j == 0:
                        act.wait_ge(sig("wkv_staged"), l + 1)
                    nc.scalar.activation(xnT[:, :], psT[:, :], ACT.Identity, bias=lns[:, 1:2], scale=lns[:, 0:1]) \
                        .then_inc(sig("xnT_ready"), 1)
                slope(0)
                slope(1)
                if attn:
                    act.wait_ge(sig("negkmax_ready"), n + 1)
                    nc.scalar.activation(expk[:, :], psT[:, :], ACT.Exp, bias=negkmax[:, j % 2:j % 2 + 1],
                                         accum_out=ksum[:, j % 2:j % 2 + 1]).then_inc(sig("expk_ready"), 1)
                slope(2)
                normalise(1, range(0, 2))
                if attn:
                    act.wait_ge(sig("tk_done"), n + 1)
                    nc.scalar.activation(expkT[:, :], psT[:, :], ACT.Copy).then_inc(sig("expkT_ready"), 1)
                slope(3)
                if attn:
                    act.wait_ge(sig("qe_ready"), n + 1)
                    nc.scalar.activation(qe[:, :], qe[:, :], ACT.Exp).then_inc(sig("expq_ready"), 1)
                slope(4)
                normalise(1, range(2, 8))
                slope(5)
                normalise(0, range(0, 2))
                slope(6)
                normalise(0, range(2, 4))
                if attn:
                    act.wait_ge(sig("tq_done"), n + 1)
                    nc.scalar.activation(qsmT[:, :], psT[:, :], ACT.Copy).then_inc(sig("qsmT_ready"), 1)
                slope(7)
                if norm2:
                    act.wait_ge(sig("t2_done"), n)
                    wait(act, "xn2_lo_ready", 2 * (n - 1))
                    if j == 1:
                        act.wait_ge(sig("ln2_staged"), l + 1)
                    nc.scalar.activation(xn2[:, :], psT[:, :], ACT.Identity, bias=lns[:, 3:4], scale=lns[:, 2:3]) \
                        .then_inc(sig("xn2_ready"), 1)
                if isinstance(n, int) and n == 0:
                    gates()

            act.wait_ge(sig("t0_done"), NBATCH)
            act.wait_ge(sig("x0_ready"), NBATCH)
            act.wait_ge(sig("ln1_shift"), NBATCH + 1)
            for t in range(4):
                nc.scalar.activation(tile(xh1[:, 0, :], t), xb(X, 0, t * P, P), ACT.Identity,
                                     bias=shift[:, 0, t:t + 1], scale=rstd[:, 0, t:t + 1]) \
                    .then_inc(sig("xh1a_ready"), 1)
            slots(act, slot)

        @block.vector
        def _(dve):
            def tile_statistics(norm, name, src, tiles=range(NT)):
                for t in tiles:
                    last = nc.vector.bn_stats(st[:, norm, t, :], src(t))
                last.then_inc(sig(name + "_st"), 1)

            def token_statistics(norm, name, st_count, count):
                dve.wait_ge(sig(name + "_st"), st_count)
                nc.vector.tensor_tensor(negmean[:, norm, :], st[:, norm, :, 1], st[:, norm, :, 4], ALU.add)
                nc.vector.tensor_tensor(sdiff[:, norm, :], st[:, norm, :, 1], st[:, norm, :, 4], ALU.subtract)
                nc.vector.tensor_tensor(sdev[:, norm, :], st[:, norm, :, 2], st[:, norm, :, 5], ALU.add) \
                    .then_inc(sig(name + "_sum"), 1)
                dve.wait_ge(sig(name + "_sum"), count)
                nc.vector.tensor_tensor(sdiff[:, norm, :], sdiff[:, norm, :], sdiff[:, norm, :], ALU.mult)
                nc.vector.tensor_scalar(negmean[:, norm, :], negmean[:, norm, :], -0.5, None, ALU.mult)
                nc.vector.tensor_scalar(sdev[:, norm, :], sdev[:, norm, :], 1.0 / D, EPS, ALU.mult, ALU.add) \
                    .then_inc(sig(name + "_sq"), 1)
                dve.wait_ge(sig(name + "_sq"), count)
                nc.vector.scalar_tensor_tensor(veps[:, norm, :], sdiff[:, norm, :], 0.25, sdev[:, norm, :],
                                               ALU.mult, ALU.add).then_inc(sig(name + "_var"), 1)

            def input_statistics(b, half):
                tile_statistics(0, "ln1", lambda t: xb(tokens, b, t * P, P), range(4 * half, 4 * half + 4))

            def input_variances(b):
                wait(dve, "ln1_shift", b)
                token_statistics(0, "ln1", 2 * b + 2, b + 1)

            def split_input(b, half):
                cols = slice(half * HALF, (half + 1) * HALF)
                wait(dve, "experts_done", 2 * NT * (b - 1) + NT * (half + 1))
                dve.wait_ge(sig("xn0T_ready"), b + 1)
                nc.vector.tensor_copy(xn2_hi[:, cols], xnT[:, cols]).then_inc(sig("xn0_hi_ready"), 1)
                dve.wait_ge(sig("xn0_hi_ready"), 2 * b + half + 1)
                nc.vector.tensor_tensor(xn2_lo[:, cols], xnT[:, cols], xn2_hi[:, cols].bitcast(F32),
                                        ALU.subtract).then_inc(sig("xn0_lo_ready"), 1)

            def route(b):
                dve.wait_ge(sig("logits_done"), b + 1)
                nc.vector.tensor_tensor(lg[:, :, :], psS[:, 0:NT * E].rearrange("p (t e) -> p t e", e=E),
                                        rb_bc[:, :].unsqueeze(1).broadcast_to([P, NT, E]), ALU.add) \
                    .then_inc(sig("lg_ready"), 1)
                dve.wait_ge(sig("lg_ready"), b + 1)
                nc.vector.tensor_reduce(lmax[:, :], lg[:, :, :], AX_X, ALU.max).then_inc(sig("lmax_ready"), 1)
                dve.wait_ge(sig("lmax_ready"), b + 1)
                nc.vector.tensor_tensor(eq[:, :, :], lg[:, :, :],
                                        lmax[:, :].unsqueeze(2).broadcast_to([P, NT, E]), ALU.is_equal) \
                    .then_inc(sig("eq_ready"), 1)
                nc.vector.tensor_tensor(lg[:, :, :], lg[:, :, :],
                                        lmax[:, :].unsqueeze(2).broadcast_to([P, NT, E]), ALU.subtract) \
                    .then_inc(sig("lsub_ready"), 1)
                dve.wait_ge(sig("eq_ready"), b + 1)
                nc.vector.tensor_tensor(eq[:, :, :], eq[:, :, :],
                                        rank[:, :].unsqueeze(1).broadcast_to([P, NT, E]), ALU.mult) \
                    .then_inc(sig("score_ready"), 1)
                dve.wait_ge(sig("score_ready"), b + 1)
                nc.vector.tensor_reduce(lmax2[:, :], eq[:, :, :], AX_X, ALU.max).then_inc(sig("lmax2_ready"), 1)
                dve.wait_ge(sig("lmax2_ready"), b + 1)
                nc.vector.tensor_tensor(eq[:, :, :], eq[:, :, :],
                                        lmax2[:, :].unsqueeze(2).broadcast_to([P, NT, E]), ALU.is_equal) \
                    .then_inc(sig("first_ready"), 1)

            def pick_weight(b):
                dve.wait_ge(sig("lexp_ready"), b + 1)
                nc.vector.tensor_reduce(lsum[:, :], le[:, :, :], AX_X, ALU.add).then_inc(sig("lsum_ready"), 1)
                dve.wait_ge(sig("lsum_ready"), b + 1)
                nc.vector.reciprocal(lrec[:, :], lsum[:, :]).then_inc(sig("lrec_ready"), 1)
                dve.wait_ge(sig("first_ready"), b + 1)
                dve.wait_ge(sig("lrec_ready"), b + 1)
                wait(dve, "pickT_done", b)
                wait(dve, "picked_act", act_products(NT) * b)
                nc.vector.tensor_tensor(pick[:, :, :], eq[:, :, :],
                                        lrec[:, :].unsqueeze(2).broadcast_to([P, NT, E]), ALU.mult) \
                    .then_inc(sig("pick_ready"), 1)
                dve.wait_ge(sig("pick_ready"), b + 1)

            def add_bias(b, half):
                dve.wait_ge(sig("ebias_done"), 2 * b + half + 1)
                wait(dve, "pool_summed", through(pool_sums, b, 4 * half + 3))
                wait(dve, "dve_summed", through(dve_sums, b, 4 * half + 3))
                nc.vector.tensor_tensor(xb(gate, b, half * HALF, HALF), xb(gate, b, half * HALF, HALF), psY[:, :],
                                        ALU.add).then_inc(sig("bias_added"), 1)

            def expert_batch(b, more):
                for t in range(NT):
                    for h in range(2):
                        if h == 1 and t in ACT_PRODUCT:
                            continue
                        dve.wait_ge(sig("experts_done"), 2 * NT * b + 2 * t + h + 1)
                        wait(dve, "dve_summed", through(dve_sums, b, t - NBUF))
                        wait(dve, "pool_summed", through(pool_sums, b, t - NBUF))
                        bank = (psM[:, h * HALF:(h + 1) * HALF], psH[:, h, :])[t % 2]
                        nc.vector.tensor_tensor(
                            ebuf[:, t % NBUF, 4 * h:4 * h + 4, :],
                            bank.rearrange("p (e d) -> p e d", d=D),
                            pick[:, t, 4 * h:4 * h + 4].unsqueeze(2).broadcast_to([P, 4, D]), ALU.mult) \
                            .then_inc(sig("picked_dve"), 1)
                    if t in DVE_SUM:
                        wait(dve, "picked_dve", through(dve_products, b, t))
                        wait(dve, "picked_act", through(act_products, b, t))
                        nc.vector.tensor_reduce(xb(gate, b, t * P, P),
                                                ebuf[:, t % NBUF, :, :].rearrange("p e d -> p d e"), AX_X, ALU.add) \
                            .then_inc(sig("dve_summed"), 1)
                    if t in (2, 4) and not (isinstance(b, int) and b == 0):
                        add_bias(b - 1, t // 2 - 1)
                    if t == 0:
                        split_input(b, 1)
                    if t in (2, 3) and more:
                        input_statistics(b + 2, t - 2)
                    if t == 4 and more:
                        input_variances(b + 2)
                    if t == 5 and more:
                        split_input(b + 1, 0)
                    if t == 6:
                        dve.wait_ge(sig("pickT_done"), b + 1)
                        nc.vector.tensor_copy(pickT[:, :], psY[0:NT * E, 0:P]).then_inc(sig("pickT_ready"), 1)
                        if more:
                            route(b + 1)
                if more:
                    pick_weight(b + 1)

            dve.wait_ge(sig("x_first_loaded"), 16)
            input_statistics(0, 0)
            input_statistics(0, 1)
            input_variances(0)
            dve.wait_ge(sig("x_loaded"), 16 * (NBATCH - 1))
            input_statistics(1, 0)
            input_statistics(1, 1)
            input_variances(1)
            nc.vector.memset(ones[:, :], 1.0)
            nc.vector.memset(eighth[:, :], 1.0 / H).then_inc(sig("ones_ready"), 1)
            dve.wait_ge(sig("ew_hi_ready"), 1)
            nc.vector.tensor_tensor(ew_lo[:, :, :], ewn[:, :, :], ew_hi[:, :, :].bitcast(F32), ALU.subtract) \
                .then_inc(sig("ew_split"), 1)
            split_input(0, 0)
            dve.wait_ge(sig("ones_ready"), 1)
            dve.wait_ge(sig("mask_ready"), 1)
            dve.wait_ge(sig("rank_ready"), E)
            dve.wait_ge(sig("router_loaded"), 32)
            route(0)
            pick_weight(0)
            dve.wait_ge(sig("x0_ready"), 1)
            batches(dve, expert_batch)

            def add_y(f, batch, half):
                dve.wait_ge(sig("y_done"), 2 * f + half + 1)
                nc.vector.tensor_tensor(xb(X, batch, half * HALF, HALF), xb(X, batch, half * HALF, HALF), psY[:, :],
                                        ALU.add).then_inc(sig("y_added"), 1)

            def normalise_rest(item, batch, par):
                dve.wait_ge(sig("ln1_shift"), NBATCH + item + 1)
                wait(dve, "g_done", item - 1)
                for t in range(4, 8):
                    last = nc.vector.tensor_scalar(tile(xh1[:, par, :], t), xb(X, batch, t * P, P),
                                                   rstd[:, 0, t:t + 1], shift[:, 0, t:t + 1], ALU.mult, ALU.add)
                last.then_inc(sig("xh1b_ready"), 1)

            def norm1_half(batch, half):
                tile_statistics(0, "ln1", lambda t: xb(X, batch, t * P, P), range(4 * half, 4 * half + 4))

            def slot(l, j):
                (attn, _), (norm2, _), (ffn, lf) = items(l, j)
                n = 4 * l + j
                f = n - 2
                par = j % 2
                fbatch = (j - 2) % 4
                nbatch = (j - 1) % 4

                def leaky(i):
                    if ffn:
                        dve.wait_ge(sig("hsl_ready"), NF * f + i + 1)
                        nc.vector.tensor_tensor(hid[:, i % NC, :], psH[:, i % 2, :], hsl[:, i % 2, :], ALU.max) \
                            .then_inc(sig("hid_ready"), 1)

                if attn and j == 0:
                    wait(dve, "k_done", n)
                    wait(dve, "ctx_done", n)
                    wait(dve, "xnT_ready", n)
                    nc.vector.tensor_copy(lns[:, 0:1], param(0, l))
                    nc.vector.tensor_copy(lns[:, 1:2], param(1, l))
                    nc.vector.tensor_copy(wk_s[:, :], of_layer(wk_all, l, 0, D))
                    nc.vector.tensor_copy(wv_s[:, :], of_layer(wv_all, l, 0, D)).then_inc(sig("wkv_staged"), 1)
                if attn and j == 1:
                    wait(dve, "xn2_ready", n - 1)
                    nc.vector.tensor_copy(lns[:, 2:3], param(2, l))
                    nc.vector.tensor_copy(lns[:, 3:4], param(3, l)).then_inc(sig("ln2_staged"), 1)
                if ffn:
                    dve.wait_ge(sig("xn2_ready"), f + 1)
                    wait(dve, "h_done", NF * f)
                    nc.vector.tensor_copy(xn2_hi[:, :], xn2[:, :]).then_inc(sig("xn2_hi_ready"), 1)
                if norm2:
                    dve.wait_ge(sig("attn_done"), n)
                    nc.vector.tensor_tensor(xb(X, nbatch), xb(X, nbatch), psM[:, :], ALU.add) \
                        .then_inc(sig("x1_added"), 1)
                last_ffn = 4 * l + j - 3
                if not isinstance(last_ffn, int) or last_ffn >= 0:
                    add_y(last_ffn, (j - 3) % 4, 1)
                if norm2:
                    dve.wait_ge(sig("x1_added"), n)
                    tile_statistics(1, "ln2", lambda t: xb(X, nbatch, t * P, P))
                leaky(0)
                if norm2:
                    wait(dve, "ln2_shift", n - 1)
                    token_statistics(1, "ln2", n, n)
                if attn:
                    dve.wait_ge(sig("k_done"), n + 1)
                    nc.vector.tensor_reduce(negkmax[:, par:par + 1], psT[:, :], AX_X, ALU.max, negate=True) \
                        .then_inc(sig("negkmax_ready"), 1)
                leaky(1)
                if attn:
                    dve.wait_ge(sig("q_done"), n + 1)
                    nc.vector.tensor_reduce(qmax[:, :], by_head(psM[:, :]), AX_X, ALU.max) \
                        .then_inc(sig("qmax_ready"), 1)
                leaky(2)
                if attn:
                    if j == 0:
                        dve.wait_ge(sig("bv_done"), l + 1)
                        nc.vector.tensor_scalar(bvm[:, :], ones[:, :], psS[:, 0:1], 1.0 / H, ALU.mult, ALU.mult) \
                            .then_inc(sig("bv_ready"), 1)
                    dve.wait_ge(sig("qmax_ready"), n + 1)
                    wait(dve, "qsm_ready", n)
                    nc.vector.tensor_tensor(by_head(qe[:, :]), by_head(psM[:, :]), over_head(qmax[:, :]),
                                            ALU.subtract).then_inc(sig("qe_ready"), 1)
                    if j == 0:
                        dve.wait_ge(sig("bias_done"), l + 1)
                        nc.vector.tensor_copy(bias_row[:, :], psS[:, 0:D]).then_inc(sig("bias_ready"), 1)
                if norm1_next(l, j):
                    wait(dve, "y_added", 2 * (n - 3) + 2)
                    norm1_half((j + 1) % 4, 1)
                leaky(3)
                if norm1_next(l, j):
                    dve.wait_ge(sig("ln1_shift"), NBATCH + n + 1)
                    token_statistics(0, "ln1", 2 * NBATCH + 2 * n + 4, NBATCH + n + 2)
                if attn:
                    dve.wait_ge(sig("expq_ready"), n + 1)
                    nc.vector.tensor_reduce(qsum[:, :], by_head(qe[:, :]), AX_X, ALU.add) \
                        .then_inc(sig("qsum_ready"), 1)
                leaky(4)
                if attn:
                    dve.wait_ge(sig("qsum_ready"), n + 1)
                    nc.vector.reciprocal(qrec[:, :], qsum[:, :]).then_inc(sig("qrec_ready"), 1)
                    nc.vector.reciprocal(krec[:, :], ksum[:, par:par + 1]).then_inc(sig("krec_ready"), 1)
                    dve.wait_ge(sig("g_done"), n + 1)
                    nc.vector.tensor_scalar(gT[:, :], psS[:, 0:D], lns[:, 0:1], None, ALU.mult) \
                        .then_inc(sig("gT_ready"), 1)
                if ffn:
                    add_y(f, fbatch, 0)
                if attn:
                    dve.wait_ge(sig("ctx_done"), n + 1)
                    nc.vector.tensor_tensor(ctxT[:, :], psS[:, 0:D], head_mask[:, :], ALU.mult) \
                        .then_inc(sig("ctx_ready"), 1)
                leaky(5)
                leaky(6)
                if attn:
                    dve.wait_ge(sig("mix_done"), n + 1)
                    dve.wait_ge(sig("krec_ready"), n + 1)
                    nc.vector.scalar_tensor_tensor(mix[:, :], psS[:, 0:D], krec[:, 0:1], bias_row[:, :],
                                                   ALU.mult, ALU.add).then_inc(sig("mix_ready"), 1)
                if norm1_next(l, j):
                    normalise_rest(n + 1, (j + 1) % 4, (j + 1) % 2)
                leaky(7)
                if not isinstance(n, int) or n + 2 < 4 * L:
                    wait(dve, "y_added", 2 * (n - 2) + 1)
                    norm1_half((j + 2) % 4, 0)
                if j == 1:
                    if attn:
                        wait(dve, "h_done", NF * (4 * l))
                        nc.vector.tensor_copy(w1_hi[:, :, :],
                                              of_layer(w1_all, l, 0, FF).rearrange("p (m c) -> p c m", c=NC)) \
                            .then_inc(sig("w1_hi_ready"), 1)

            dve.wait_ge(sig("param_loaded"), 16 * 2)
            dve.wait_ge(sig("attn_loaded"), 16 * 4 * L)
            dve.wait_ge(sig("ffn_loaded"), 16 * 2 * L)
            dve.wait_ge(sig("x0_ready"), NBATCH)
            norm1_half(1, 0)
            normalise_rest(0, 0, 0)
            for half in range(2):
                add_bias(NBATCH - 1, half)
            slots(dve, slot)
            add_y(4 * L - 1, 3, 1)
            dve.wait_ge(sig("gate_ready"), 1)
            for b in range(NBATCH):
                if b == NBATCH - 1:
                    dve.wait_ge(sig("y_added"), 2 * 4 * L)
                nc.vector.tensor_tensor(gate[:, b, :], gate[:, b, :], X[:, b, :], ALU.mult) \
                    .then_inc(sig("gated"), 1)

        @block.gpsimd
        def _(pool):
            nc.gpsimd.memset(ident[:, :], 0.0).then_inc(sig("const_ready"), 1)
            nc.gpsimd.memset(head_mask[:, :], 1.0).then_inc(sig("const_ready"), 1)
            nc.gpsimd.memset(minus_half[:, :], -0.5).then_inc(sig("const_ready"), 1)
            nc.gpsimd.memset(eb_diag[:, :, :], 0.0).then_inc(sig("const_ready"), 1)
            pool.wait_ge(sig("const_ready"), 4)
            nc.gpsimd.affine_select(out=ident[:, :], in_=ident[:, :], compare_op=ALU.not_equal, fill=1.0, base=0,
                                    pattern=[[-1, P]], channel_multiplier=1).then_inc(sig("const_ready"), 1)
            for t in range(NT):
                pool.dma_start(eb_diag[E * t:E * (t + 1), t, :], expert_b).then_inc(sig("eb_loaded"), 16)
            by = head_mask[:, :].rearrange("p (g d) -> p g d", d=DH)
            nc.gpsimd.affine_select(out=by, in_=by, compare_op=ALU.is_ge, fill=0.0, base=0,
                                    pattern=[[-DH, H], [0, DH]], channel_multiplier=1) \
                .then_inc(sig("mask_step"), 1)
            pool.wait_ge(sig("mask_step"), 1)
            nc.gpsimd.affine_select(out=by, in_=by, compare_op=ALU.is_ge, fill=0.0, base=DH - 1,
                                    pattern=[[DH, H], [0, DH]], channel_multiplier=-1) \
                .then_inc(sig("mask_ready"), 1)
            for e in range(E):
                nc.gpsimd.memset(rank[:, e:e + 1], float(E - e)).then_inc(sig("rank_ready"), 1)

            def reciprocal_deviations(norm, name, count):
                pool.wait_ge(sig(name + "_var"), count)
                nc.gpsimd.tensor_tensor(rstd[:, norm, :], veps[:, norm, :], minus_half[:, :], ALU.pow) \
                    .then_inc(sig(name + "_rstd"), 1)
                pool.wait_ge(sig(name + "_rstd"), count)
                nc.gpsimd.tensor_tensor(shift[:, norm, :], negmean[:, norm, :], rstd[:, norm, :], ALU.mult) \
                    .then_inc(sig(name + "_shift"), 1)

            def expert_batch(b, more):
                for t in range(NT):
                    if t in DVE_SUM:
                        continue
                    wait(pool, "picked_dve", through(dve_products, b, t))
                    wait(pool, "picked_act", through(act_products, b, t))
                    a = ebuf[:, t % NBUF, :, :]
                    nc.gpsimd.tensor_tensor(a[:, 0:4, :], a[:, 0:4, :], a[:, 4:8, :], ALU.add) \
                        .then_inc(sig("sum4"), 1)
                    wait(pool, "sum4", through(pool_sums, b, t))
                    nc.gpsimd.tensor_tensor(a[:, 0:2, :], a[:, 0:2, :], a[:, 2:4, :], ALU.add) \
                        .then_inc(sig("sum2"), 1)
                    wait(pool, "sum2", through(pool_sums, b, t))
                    nc.gpsimd.tensor_tensor(xb(gate, b, t * P, P), a[:, 0, :], a[:, 1, :], ALU.add) \
                        .then_inc(sig("pool_summed"), 1)
                    if more and t == 4:
                        pool.wait_ge(sig("xh0_ready"), b + 2)
                        reciprocal_deviations(0, "ln1", b + 3)

            def slot(l, j):
                (attn, _), (norm2, _), (ffn, _) = items(l, j)
                n = 4 * l + j
                f = n - 2
                if ffn:
                    pool.wait_ge(sig("xn2_hi_ready"), f + 1)
                    for h in range(2):
                        cols = slice(h * HALF, (h + 1) * HALF)
                        nc.gpsimd.tensor_tensor(xn2_lo[:, cols], xn2[:, cols], xn2_hi[:, cols].bitcast(F32),
                                                ALU.subtract).then_inc(sig("xn2_lo_ready"), 1)
                if norm2:
                    wait(pool, "xh2_ready", NT * (n - 1))
                    reciprocal_deviations(1, "ln2", n)
                if norm1_next(l, j):
                    pool.wait_ge(sig("xh1a_ready"), 4 * (n + 1))
                    pool.wait_ge(sig("xh1b_ready"), n + 1)
                    reciprocal_deviations(0, "ln1", NBATCH + n + 2)
                if attn:
                    pool.wait_ge(sig("qrec_ready"), n + 1)
                    wait(pool, "tq_done", n)
                    nc.gpsimd.tensor_tensor(by_head(qsm[:, :]), by_head(qe[:, :]), over_head(qrec[:, :]), ALU.mult) \
                        .then_inc(sig("qsm_ready"), 1)
                if attn and j == 1:
                    pool.wait_ge(sig("w1_hi_ready"), l + 1)
                    nc.gpsimd.tensor_tensor(w1_lo[:, :, :],
                                            of_layer(w1_all, l, 0, FF).rearrange("p (m c) -> p c m", c=NC),
                                            w1_hi[:, :, :].bitcast(F32), ALU.subtract).then_inc(sig("w1_staged"), 1)

            reciprocal_deviations(0, "ln1", 1)
            pool.wait_ge(sig("xh0_ready"), 1)
            reciprocal_deviations(0, "ln1", 2)
            batches(pool, expert_batch)
            slots(pool, slot)
            for b in range(NBATCH):
                pool.wait_ge(sig("gated"), b + 1)
                nc.gpsimd.tensor_tensor(xraw[:, b, :], xraw[:, b, :], gate[:, b, :], ALU.add) \
                    .then_inc(sig("out_ready"), 1)


_OUTS = [((4, 1024, 128), 'float32')]


def kernel(**inputs):
    import numpy as _np
    import concourse.bacc as _bacc
    from concourse import mybir as _mybir
    from concourse.bass_utils import run_bass_kernel_spmd as _run

    a = {k[3:]: _np.asarray(v) for k, v in inputs.items()}
    laid_out = {
        "x": a["attn_x"],
        "ln_params": _np.stack([a[f"attn_{k}"].T for k in ("ln1_w", "ln1_b", "ln2_w", "ln2_b")], axis=1),
        "wq": a["attn_wq"], "wk": a["attn_wk"], "wv": a["attn_wv"], "wo": a["attn_wo"], "bo": a["attn_bo"],
        "w1": a["attn_w1"], "w2": a["attn_w2"],
        "router_wT": a["ffn_router_w"].T, "router_b": a["ffn_router_b"],
        "expert_wT": a["ffn_expert_w"].transpose(2, 0, 1), "expert_b": a["ffn_expert_b"],
    }
    nc = _bacc.Bacc("TRN2", target_bir_lowering=False, num_devices=1)
    arrays, args = {}, []
    for name, value in laid_out.items():
        value = _np.ascontiguousarray(value)
        arrays[f"in_{name}_dram"] = value
        args.append(nc.dram_tensor(f"in_{name}_dram", value.shape, _mybir.dt.from_np(value.dtype),
                                   kind="ExternalInput").ap())
    for i, (shape, dtype) in enumerate(_OUTS):
        dt = _mybir.dt.from_np(_np.dtype(dtype))
        args.append(nc.dram_tensor(f"out_{i}_dram", shape, dt, kind="ExternalOutput").ap())
    build_program(nc, *args)
    r = _run(nc, [arrays], core_ids=[0])
    return r.results[0]["out_0_dram"]
```

```python
from contextlib import ExitStack

import concourse.bass as bass
from concourse import mybir

ALU = mybir.AluOpType
ACT = mybir.ActivationFunctionType
AX_X = mybir.AxisListType.X
F32 = mybir.dt.float32
F32R = mybir.dt.float32r
I32 = mybir.dt.int32

EPS = 1e-5
SLOPE = 0.01


def build_program(nc, x_in, ln_params, wq, wk, wv, wo, bo, w1, w2, router_wT, router_b, expert_wT, expert_b, out):
    NBATCH, T, D = x_in.shape
    L = wq.shape[0]
    FF = w1.shape[2]
    E = router_wT.shape[1]
    H = 8
    DH = D // H
    P = 128
    NT = T // P
    HALF = T // 2
    NC = FF // P
    NF = 2 * NC
    assert NBATCH == 4 and D == P and NT == 8 and NC == 4 and E == 8

    with ExitStack() as ctx:
        def sb(name, shape, dt=F32):
            return ctx.enter_context(nc.sbuf_tensor(name, shape, dt))

        def ps(name, shape):
            return ctx.enter_context(nc.psum_tensor(name, shape, F32))

        def sem(name):
            return ctx.enter_context(nc.semaphore(name))

        psT = ps("psT", [P, T])
        psM = ps("psM", [P, T])
        psY = ps("psY", [P, HALF])
        psS = ps("psS", [P, HALF])
        psH = ps("psH", [P, 2, HALF])

        xraw = sb("xraw", [P, NBATCH, T])
        X = sb("X", [P, NBATCH, T])
        gate = sb("gate", [P, NBATCH, T])
        wq_all = sb("wq_all", [P, L, D])
        wk_all = sb("wk_all", [P, L, D])
        wv_all = sb("wv_all", [P, L, D])
        wo_all = sb("wo_all", [P, L, D])
        w1_all = sb("w1_all", [P, L, FF])
        w2_all = sb("w2_all", [P, L, NC, D])
        lnp = sb("lnp", [P, 4, L])
        lns = sb("lns", [P, 4])
        bo_row = sb("bo_row", [1, L, D])
        wk_s = sb("wk_s", [P, D])
        wv_s = sb("wv_s", [P, D])
        w1_hi = sb("w1_hi", [P, NC, P], F32R)
        w1_lo = sb("w1_lo", [P, NC, P], F32R)
        ident = sb("ident", [P, P])
        head_mask = sb("head_mask", [P, P])
        ones = sb("ones", [P, P])
        eighth = sb("eighth", [1, P])
        minus_half = sb("minus_half", [P, NT])
        rank = sb("rank", [P, E])
        st = sb("st", [P, 2, NT, 6])
        sdiff = sb("sdiff", [P, 2, NT])
        sdev = sb("sdev", [P, 2, NT])
        negmean = sb("negmean", [P, 2, NT])
        veps = sb("veps", [P, 2, NT])
        rstd = sb("rstd", [P, 2, NT])
        shift = sb("shift", [P, 2, NT])
        xh1 = sb("xh1", [P, 2, T])
        xnT = sb("xnT", [P, T])
        negkmax = sb("negkmax", [P, 2])
        ksum = sb("ksum", [P, 2])
        krec = sb("krec", [P, 1])
        expk = sb("expk", [P, T])
        expkT = sb("expkT", [P, T])
        qmax = sb("qmax", [P, NT * H])
        qsum = sb("qsum", [P, NT * H])
        qrec = sb("qrec", [P, NT * H])
        qe = sb("qe", [P, T])
        qsm = sb("qsm", [P, T])
        qsmT = sb("qsmT", [P, T])
        gT = sb("gT", [P, D])
        ctxT = sb("ctxT", [P, D])
        mix = sb("mix", [P, D])
        bvm = sb("bvm", [P, D])
        bias_row = sb("bias_row", [P, D])
        xh2 = sb("xh2", [P, T])
        xn2 = sb("xn2", [P, T])
        xn2_hi = sb("xn2_hi", [P, T], F32R)
        xn2_lo = sb("xn2_lo", [P, T], F32R)
        hsl = sb("hsl", [P, 2, HALF])
        hid = sb("hid", [P, NC, HALF])
        ewn = sb("ewn", [P, E, D])
        ew_hi = sb("ew_hi", [P, E, D], F32R)
        ew_lo = sb("ew_lo", [P, E, D], F32R)
        rwT = sb("rwT", [P, E])
        rb_bc = sb("rb_bc", [P, E])
        eb_diag = sb("eb_diag", [NT * E, NT, D])
        lg = sb("lg", [P, NT, E])
        lmax = sb("lmax", [P, NT])
        eq = sb("eq", [P, NT, E])
        lmax2 = sb("lmax2", [P, NT])
        pick = sb("pick", [P, 2, NT, E])
        le = sb("le", [P, NT, E])
        lsum = sb("lsum", [P, NT])
        lrec = sb("lrec", [P, NT])
        pickT = sb("pickT", [NT * E, P])
        NBUF = 4
        ebuf = sb("ebuf", [P, NBUF, E, D])

        WARM_UP = 64
        DVE_SUM = ((3, 7), (3,), (7,), (6, 7))

        def expert_tokens(b):
            return xnT[:, :] if b < 2 else hid[:, 2 * b - 4:2 * b - 2, :].rearrange("p c t -> p (c t)")

        def expert_bank(b, t, half):
            if b < 2 and t % 2 == 0:
                return psM[:, half * HALF:(half + 1) * HALF]
            return psH[:, half, :]

        def dve_sums(b, t):
            return sum(len(tiles) for tiles in DVE_SUM[:b]) + sum(u <= t for u in DVE_SUM[b])

        def pool_sums(b, t):
            return NT * b + t + 1 - dve_sums(b, t)

        def summed_before(b, t):
            b, t = (b, t - NBUF) if t >= NBUF else (b - 1, t - NBUF + NT)
            return ("dve_summed", dve_sums(b, t)) if t in DVE_SUM[b] else ("pool_summed", pool_sums(b, t))

        S = {}

        def sig(name):
            if name not in S:
                S[name] = sem(name)
            return S[name]

        def wait(eng, name, value):
            if isinstance(value, int) and value <= 0:
                return
            eng.wait_ge(sig(name), value)

        def parts(f):
            if isinstance(f, int) and f == 4 * L - 1:
                return [a[:, :, :].rearrange("p e d -> p (e d)") for a in (ew_hi, ew_lo)]
            return xn2_hi[:, :], xn2_lo[:, :]

        def emptying(n, k):
            return isinstance(n, int) and n == 4 * L + k

        def tile(a, t):
            return a[:, t * P:(t + 1) * P]

        def by_head(a):
            return a.rearrange("p (g d) -> p g d", d=DH)

        def over_head(a):
            return a.unsqueeze(2).broadcast_to([P, NT * H, DH])

        def xb(a, b, lo=0, n=T):
            if isinstance(b, int):
                return a[:, b, lo:lo + n]
            return a[:, :, :].rearrange("p b t -> p (b t)")[:, bass.ds(b * T + lo, n)]

        def of_layer(a, l, lo, n):
            flat = a[:, :, :, :].rearrange("p l c d -> p (l c d)") if len(a.shape) == 4 \
                else a[:, :, :].rearrange("p l d -> p (l d)")
            w = flat.shape[1] // L
            if isinstance(l, int):
                return flat[:, l * w + lo:l * w + lo + n]
            return flat[:, bass.ds(l * w + lo, n)]

        def param(k, l):
            if isinstance(l, int):
                return lnp[:, k, l:l + 1]
            return lnp[:, k, bass.ds(l, 1)]

        def slots(eng, slot):
            for j in range(4):
                slot(0, j)
            with eng.Fori(1, L) as l:
                for j in range(4):
                    slot(l, j)
            for j in range(2):
                slot(L, j)

        def items(l, j):
            def there(lag):
                if isinstance(l, int):
                    n = 4 * l + j - lag
                    return 0 <= n < 4 * L
                return True
            return (there(0), l), (there(1), l if j >= 1 else l - 1), (there(2), l if j >= 2 else l - 1)

        def norm1_next(l, j):
            n = 4 * l + j
            return not isinstance(n, int) or n + 1 < 4 * L

        block = ctx.enter_context(nc.Block())

        @block.sync
        def _(sp):
            sp.dma_start(xraw[:, 0, :], x_in[0].rearrange("(p t) d -> p (t d)", p=P)) \
                .then_inc(sig("x_first_loaded"), 16)
            sp.dma_start(ewn[:, :, :], expert_wT).then_inc(sig("expert_loaded"), 16)
            for b in range(1, NBATCH):
                sp.dma_start(xraw[:, b, :], x_in[b].rearrange("(p t) d -> p (t d)", p=P)) \
                    .then_inc(sig("x_loaded"), 16)
            sp.wait_ge(sig("eb_zeroed"), 1)
            for t in range(NT):
                sp.dma_start(eb_diag[E * t:E * (t + 1), t, :], expert_b).then_inc(sig("eb_loaded"), 16)
            for l in range(L):
                sp.dma_start(wk_all[:, l, :], wk[l]).then_inc(sig("attn_loaded"), 16)
                sp.dma_start(wq_all[:, l, :], wq[l]).then_inc(sig("attn_loaded"), 16)
                sp.dma_start(wv_all[:, l, :], wv[l]).then_inc(sig("attn_loaded"), 16)
                sp.dma_start(wo_all[:, l, :], wo[l]).then_inc(sig("attn_loaded"), 16)
                sp.dma_start(w1_all[:, l, :], w1[l]).then_inc(sig("ffn_loaded"), 16)
                sp.dma_start(w2_all[:, l, :, :], w2[l].rearrange("(p c) d -> p c d", c=NC)) \
                    .then_inc(sig("ffn_loaded"), 16)
            for b in range(NBATCH - 1):
                sp.wait_ge(sig("out_ready"), b + 1)
                sp.dma_start(out[b].rearrange("(p t) d -> p (t d)", p=P), xraw[:, b, :]) \
                    .then_inc(sig("stored"), 16)
            for half in range(2):
                sp.wait_ge(sig("last_out_ready"), half + 1)
                cols = slice(half * HALF, (half + 1) * HALF)
                sp.dma_start(out[NBATCH - 1].rearrange("(p t) d -> p (t d)", p=P)[:, cols],
                             xraw[:, NBATCH - 1, cols]).then_inc(sig("stored"), 16)
            sp.wait_ge(sig("stored"), 16 * (NBATCH + 1))

        @block.tensor
        def _(pe):
            def transposes(dst, src):
                for t in range(NT):
                    last = nc.tensor.transpose(tile(dst, t), tile(src, t), ident[:, :])
                return last

            def split_product(dst, hi_w, lo_w, hi_x, lo_x):
                nc.tensor.matmul(dst, hi_w, hi_x, start=True, stop=False)
                nc.tensor.matmul(dst, lo_w, hi_x, start=False, stop=False)
                return nc.tensor.matmul(dst, hi_w, lo_x, start=False, stop=True)

            def normalised_tiles(b):
                pe.wait_ge(sig("const_ready"), 4)
                pe.wait_ge(sig("xh0_ready"), b + 1)
                wait(pe, "xn0T_ready", b)
                transposes(psT, xh1[:, b % 2, :]).then_inc(sig("t0_done"), 1)

            def logits(b):
                pe.wait_ge(sig("router_loaded"), 32)
                pe.wait_ge(sig("xn0T_ready"), b + 1)
                wait(pe, "lg_ready", b)
                for t in range(NT):
                    last = nc.tensor.matmul(psS[:, t * E:(t + 1) * E], tile(expert_tokens(b), t), rwT[:, :],
                                            start=True, stop=True)
                last.then_inc(sig("logits_done"), 1)

            def picked_bias(b, half):
                pe.wait_ge(sig("pickT_ready"), b + 1)
                wait(pe, "bias_added", 2 * b + half)
                for t in range(4):
                    last = nc.tensor.matmul(tile(psY, t), pickT[:, :], eb_diag[:, 4 * half + t, :],
                                            start=True, stop=True)
                last.then_inc(sig("ebias_done"), 1)

            def expert_step(b, t):
                if t % 4 == 0:
                    pe.wait_ge(sig("xn0_lo_ready"), 2 * b + t // 4 + 1)
                before = t - 1 if b >= 2 else t - 2
                for h, picked in enumerate(("picked_dve", "picked_act")):
                    wait(pe, picked, NT * b + before + 1)
                    split_product(expert_bank(b, t, h), tile(xn2_hi, t), tile(xn2_lo, t),
                                  ew_hi[:, 4 * h:4 * h + 4, :], ew_lo[:, 4 * h:4 * h + 4, :]) \
                        .then_inc(sig("experts_done"), 1)
                if t in (1, 3) and b > 0:
                    picked_bias(b - 1, t // 2)
                if t == 5:
                    pe.wait_ge(sig("const_ready"), 4)
                    wait(pe, "bias_added", 2 * b)
                    nc.tensor.transpose(psY[0:NT * E, 0:P], pick[:, b % 2, :, :].rearrange("p t e -> p (t e)"),
                                        ident[:, :]).then_inc(sig("pickT_done"), 1)

            pe.wait_ge(sig("const_ready"), 4)
            for t in range(WARM_UP):
                nc.tensor.transpose(psM[:, 0:P], ident[:, :], ident[:, :])
            normalised_tiles(0)
            logits(0)
            pe.wait_ge(sig("ew_split"), 1)
            for b in range(2):
                for t in range(NT):
                    expert_step(b, t)
                    if b == 0 and t == 1:
                        normalised_tiles(1)
                        pe.wait_ge(sig("eb_loaded"), 16 * NT)
                    if b == 0 and t == 3:
                        logits(1)
                    if b == 1 and t == 0:
                        normalised_tiles(2)
                    if b == 1 and t == 2:
                        logits(2)
                    if b == 1 and t == 4:
                        normalised_tiles(3)
            logits(3)

            def w1_step(f, i):
                half, c = i // NC, i % NC
                if isinstance(f, int) and f == 0 and i < 2:
                    pe.wait_ge(sig(("picked_dve", "picked_act")[i]), NT * NBATCH)
                if c == 0:
                    pe.wait_ge(sig("xn2_lo_ready"), 2 * f + half + 1)
                wait(pe, "hid_ready", NF * f + i - 1)
                cols = slice(half * HALF, (half + 1) * HALF)
                hi, lo = parts(f)
                split_product(psH[:, i % 2, :], w1_hi[:, c, :], w1_lo[:, c, :], hi[:, cols], lo[:, cols]) \
                    .then_inc(sig("h_done"), 1)

            def w2_step(f, l, i):
                c = i % NC
                pe.wait_ge(sig("hid_ready"), NF * f + i + 1)
                if isinstance(f, int) and f == 0 and i == 0:
                    pe.wait_ge(sig("bias_added"), 2 * NBATCH)
                if c == 0:
                    wait(pe, "y_added", 2 * f + i // NC)
                for t in range(4):
                    last = nc.tensor.matmul(tile(psY, t), tile(hid[:, i % NC, :], t), of_layer(w2_all, l, c * D, D),
                                            start=(c == 0 and t == 0), stop=(c == NC - 1), skip_group_check=True)
                if c == NC - 1:
                    last.then_inc(sig("y_done"), 1)

            def norm2_transposes(n, attn):
                if attn:
                    wait(pe, "xh2_ready", NT * n)
                    pe.wait_ge(sig("qsmT_ready"), n + 1)
                else:
                    pe.wait_ge(sig("xh2_ready"), NT * (n - 1) + 4)
                    pe.wait_ge(sig("xh2b_ready"), 1)
                transposes(psT, xh2).then_inc(sig("t2_done"), 1)

            def slot(l, j):
                (attn, _), (norm2, _), (ffn, lf) = items(l, j)
                n = 4 * l + j
                f = n - 2

                def ffn_step(i):
                    if ffn:
                        if i < NF and not (emptying(n, 1) and i == 0):
                            if i == 0 and j == 2:
                                pe.wait_ge(sig("w1_staged"), l + 1)
                            w1_step(f, i)
                        if i >= 2:
                            w2_step(f, lf, i - 2)
                    elif attn and i < NT:
                        expert_step(n + 2, i)
                    elif attn and n == 1:
                        picked_bias(NBATCH - 1, i - NT)

                ffn_step(0)
                ffn_step(1)
                if attn:
                    pe.wait_ge(sig("xnT_ready"), n + 1)
                    if j == 0:
                        pe.wait_ge(sig("wkv_staged"), l + 1)
                    for h in (0, 1):
                        last = nc.tensor.matmul(psT[:, h * HALF:(h + 1) * HALF], wk_s[:, :],
                                                xnT[:, h * HALF:(h + 1) * HALF], start=True, stop=True)
                    last.then_inc(sig("k_done"), 1)
                    wait(pe, "x1_added", n)
                    for t in range(NT):
                        last = nc.tensor.matmul(tile(psM, t), tile(xnT, t), of_layer(wq_all, l, 0, D),
                                                start=True, stop=True)
                    last.then_inc(sig("q_done"), 1)
                    if j == 0:
                        wait(pe, "mix_ready", n)
                        pe.wait_ge(sig("lg_ready"), NBATCH)
                        nc.tensor.matmul(psS[:, 0:1], wv_s[:, :], lns[:, 1:2], start=True, stop=True) \
                            .then_inc(sig("bv_done"), 1)
                ffn_step(2)
                if attn:
                    pe.wait_ge(sig("expk_ready"), n + 1)
                    transposes(psT, expk).then_inc(sig("tk_done"), 1)
                    if j == 0:
                        pe.wait_ge(sig("bv_ready"), l + 1)
                        nc.tensor.matmul(psS[:, 0:D], bvm[:, :], of_layer(wo_all, l, 0, D), start=True, stop=False)
                        nc.tensor.matmul(psS[:, 0:D], eighth[:, :], of_layer(bo_row, l, 0, D),
                                         start=False, stop=True).then_inc(sig("bias_done"), 1)
                ffn_step(3)
                ffn_step(4)
                if attn:
                    pe.wait_ge(sig("expkT_ready"), n + 1)
                    wait(pe, "mix_ready", n)
                    pe.wait_ge(sig("bias_ready"), l + 1)
                    for t in range(NT):
                        last = nc.tensor.matmul(psS[:, 0:D], tile(xh1[:, j % 2, :], t), tile(expkT, t),
                                                start=(t == 0), stop=(t == NT - 1))
                    last.then_inc(sig("g_done"), 1)
                ffn_step(5)
                if emptying(n, 0):
                    norm2_transposes(n, attn)
                if attn:
                    pe.wait_ge(sig("gT_ready"), n + 1)
                    nc.tensor.matmul(psS[:, 0:D], wv_s[:, :], gT[:, :], start=True, stop=True) \
                        .then_inc(sig("ctx_done"), 1)
                ffn_step(6)
                if attn:
                    pe.wait_ge(sig("ctx_ready"), n + 1)
                    nc.tensor.matmul(psS[:, 0:D], ctxT[:, :], of_layer(wo_all, l, 0, D), start=True, stop=True) \
                        .then_inc(sig("mix_done"), 1)
                    pe.wait_ge(sig("qsm_ready"), n + 1)
                    transposes(psT, qsm).then_inc(sig("tq_done"), 1)
                ffn_step(7)
                if norm2 and attn:
                    norm2_transposes(n, attn)
                if attn:
                    pe.wait_ge(sig("mix_ready"), n + 1)
                    pe.wait_ge(sig("qsmT_ready"), n + 1)
                    pe.wait_ge(sig("qe_ready"), n + 1)
                    for t in range(NT):
                        last = nc.tensor.matmul(tile(psM, t), tile(qsmT, t), mix[:, :], start=True, stop=True)
                    last.then_inc(sig("attn_done"), 1)
                ffn_step(8)
                if norm1_next(l, j):
                    pe.wait_ge(sig("xh1a_ready"), 4 * (n + 2))
                    pe.wait_ge(sig("xh1b_ready"), n + 2)
                    pe.wait_ge(sig("qsmT_ready"), n + 1)
                    wait(pe, "xn2_ready", n)
                    transposes(psT, xh1[:, (j + 1) % 2, :]).then_inc(sig("t1_done"), 1)
                if emptying(n, 0):
                    w1_step(f + 1, 0)
                ffn_step(9)

            pe.wait_ge(sig("ffn_loaded"), 16 * 2 * L)
            pe.wait_ge(sig("attn_loaded"), 16 * 4 * L)
            pe.wait_ge(sig("param_loaded"), 16 * 2)
            pe.wait_ge(sig("ones_ready"), 1)
            pe.wait_ge(sig("xn0T_ready"), NBATCH)
            pe.wait_ge(sig("xh1a_ready"), 4)
            pe.wait_ge(sig("xh1b_ready"), 1)
            transposes(psT, xh1[:, 0, :]).then_inc(sig("t1_done"), 1)
            slots(pe, slot)

        @block.scalar
        def _(act):
            act.dma_start(rwT[:, :], router_wT).then_inc(sig("router_loaded"), 16)
            act.dma_start(rb_bc[:, :], router_b.rearrange("(a e) -> a e", a=1).broadcast_to([P, E])) \
                .then_inc(sig("router_loaded"), 16)
            act.dma_start(lnp[:, :, :], ln_params).then_inc(sig("param_loaded"), 16)
            act.dma_start(bo_row[:, :, :], bo.rearrange("l (a d) -> a l d", a=1)).then_inc(sig("param_loaded"), 16)

            def normalise_input(b, tiles):
                k = b % 2
                if tiles.start == 0:
                    act.wait_ge(sig("in_shift"), b + 1)
                    wait(act, "t0_done", b - 1)
                    wait(act, "x0_ready", b - 1)
                for t in tiles:
                    last = nc.scalar.activation(tile(xh1[:, k, :], t), xb(xraw, b, t * P, P), ACT.Identity,
                                                bias=shift[:, k, t:t + 1], scale=rstd[:, k, t:t + 1])
                if tiles.stop == NT:
                    last.then_inc(sig("xh0_ready"), 1)

            def residual_stream(b):
                act.wait_ge(sig("xh0_ready"), b + 1)
                nc.scalar.activation(xb(X, b), xh1[:, b % 2, :], ACT.Copy).then_inc(sig("x0_ready"), 1)

            def feature_major(b):
                act.wait_ge(sig("t0_done"), b + 1)
                if b < 2:
                    wait(act, "xn0_lo_ready", 2 * b)
                nc.scalar.activation(expert_tokens(b), psT[:, :], ACT.Copy).then_inc(sig("xn0T_ready"), 1)

            def router_exponentials(b):
                act.wait_ge(sig("lsub_ready"), b + 1)
                nc.scalar.activation(le[:, :, :], lg[:, :, :], ACT.Exp).then_inc(sig("lexp_ready"), 1)

            def expert_step(b, t):
                act.wait_ge(sig("experts_done"), 2 * NT * b + 2 * t + 2)
                act.wait_ge(sig("pick_ready"), b + 1)
                if NT * b + t >= NBUF:
                    name, count = summed_before(b, t)
                    act.wait_ge(sig(name), count)
                for e in range(4):
                    last = nc.scalar.activation(ebuf[:, t % NBUF, 4 + e, :], tile(expert_bank(b, t, 1), e), ACT.Copy,
                                                scale=pick[:, b % 2, t, 4 + e:5 + e])
                last.then_inc(sig("picked_act"), 1)

            normalise_input(0, range(NT))
            act.wait_ge(sig("expert_loaded"), 16)
            nc.scalar.activation(ew_hi[:, :, :], ewn[:, :, :], ACT.Copy) \
                .then_inc(sig("ew_hi_ready"), 1)
            feature_major(0)
            normalise_input(1, range(0, 4))
            router_exponentials(0)
            normalise_input(1, range(4, NT))
            for b in range(2):
                for t in range(NT):
                    expert_step(b, t)
                    if b == 0 and t == 0:
                        residual_stream(0)
                    if b == 0 and t == 1:
                        feature_major(1)
                        residual_stream(1)
                    if b == 0 and t in (3, 5, 6):
                        k = (3, 5, 6).index(t)
                        normalise_input(2, range(3 * k, min(3 * k + 3, NT)))
                    if b == 0 and t == 4:
                        router_exponentials(1)
                    if b == 1 and t < 3:
                        normalise_input(3, range(3 * t, min(3 * t + 3, NT)))
                    if b == 1 and t == 0:
                        feature_major(2)
                    if b == 1 and t == 3:
                        residual_stream(2)
                    if b == 1 and t == 4:
                        router_exponentials(2)
                    if b == 1 and t == 5:
                        feature_major(3)
                    if b == 1 and t == 6:
                        act.wait_ge(sig("t0_done"), 3)
                        act.wait_ge(sig("x0_ready"), 3)
                        act.wait_ge(sig("ln1_shift"), 1)
                        for k in range(4):
                            nc.scalar.activation(tile(xh1[:, 0, :], k), xb(X, 0, k * P, P), ACT.Identity,
                                                 bias=shift[:, 0, k:k + 1], scale=rstd[:, 0, k:k + 1]) \
                                .then_inc(sig("xh1a_ready"), 1)

            residual_stream(3)
            act.wait_ge(sig("x0_ready"), NBATCH)
            router_exponentials(3)

            def silu(b):
                act.wait_ge(sig("bias_added"), 2 * NBATCH)
                nc.scalar.activation(gate[:, b, :], gate[:, b, :], ACT.Silu).then_inc(sig("gate_ready"), 1)

            def slot(l, j):
                (attn, _), (norm2, _), (ffn, _) = items(l, j)
                n = 4 * l + j
                f = n - 2

                def slope(i):
                    if ffn:
                        act.wait_ge(sig("h_done"), NF * f + i + 1)
                        nc.scalar.activation(hsl[:, i % 2, :], psH[:, i % 2, :], ACT.Copy, scale=SLOPE) \
                            .then_inc(sig("hsl_ready"), 1)
                    elif attn:
                        expert_step(n + 2, i)

                def normalise(norm, tiles):
                    if not (norm2, norm1_next(l, j))[norm == 0]:
                        return
                    if tiles.start == 0 and norm == 0:
                        act.wait_ge(sig("ln1_shift"), n + 2)
                        wait(act, "g_done", n)
                    elif tiles.start == 0:
                        wait(act, "ln2_shift", n)
                        wait(act, "t2_done", n - 1)
                    dst = xh1[:, (j + 1) % 2, :] if norm == 0 else xh2
                    batch = (j + 1) % 4 if norm == 0 else (j - 1) % 4
                    for t in tiles:
                        nc.scalar.activation(tile(dst, t), xb(X, batch, t * P, P), ACT.Identity,
                                             bias=shift[:, norm, t:t + 1], scale=rstd[:, norm, t:t + 1]) \
                            .then_inc(sig(("xh1a_ready", "xh2_ready")[norm]), 1)

                def feature_major_norm2():
                    act.wait_ge(sig("t2_done"), n)
                    wait(act, "xn2_lo_ready", 2 * (n - 1))
                    if j == 1:
                        act.wait_ge(sig("ln2_staged"), l + 1)
                    nc.scalar.activation(xn2[:, :], psT[:, :], ACT.Identity, bias=lns[:, 3:4], scale=lns[:, 2:3]) \
                        .then_inc(sig("xn2_ready"), 1)

                if attn:
                    act.wait_ge(sig("t1_done"), n + 1)
                    wait(act, "q_done", n)
                    if j == 0:
                        act.wait_ge(sig("wkv_staged"), l + 1)
                    nc.scalar.activation(xnT[:, :], psT[:, :], ACT.Identity, bias=lns[:, 1:2], scale=lns[:, 0:1]) \
                        .then_inc(sig("xnT_ready"), 1)
                slope(0)
                slope(1)
                if emptying(n, 1):
                    silu(1)
                if attn:
                    act.wait_ge(sig("negkmax_ready"), n + 1)
                    nc.scalar.activation(expk[:, :], psT[:, :], ACT.Exp, bias=negkmax[:, j % 2:j % 2 + 1],
                                         accum_out=ksum[:, j % 2:j % 2 + 1]).then_inc(sig("expk_ready"), 1)
                slope(2)
                if emptying(n, 1):
                    silu(2)
                    silu(3)
                if emptying(n, 0):
                    silu(0)
                else:
                    normalise(1, range(0, 2))
                if attn:
                    act.wait_ge(sig("tk_done"), n + 1)
                    nc.scalar.activation(expkT[:, :], psT[:, :], ACT.Copy).then_inc(sig("expkT_ready"), 1)
                slope(3)
                if attn:
                    act.wait_ge(sig("qe_ready"), n + 1)
                    nc.scalar.activation(qe[:, :], qe[:, :], ACT.Exp).then_inc(sig("expq_ready"), 1)
                slope(4)
                normalise(1, range(0, 4) if emptying(n, 0) else range(2, 8 if ffn else 5))
                slope(5)
                if not ffn:
                    normalise(1, range(5, 8))
                if emptying(n, 0):
                    feature_major_norm2()
                normalise(0, range(0, 2))
                slope(6)
                normalise(0, range(2, 4))
                if attn:
                    act.wait_ge(sig("tq_done"), n + 1)
                    nc.scalar.activation(qsmT[:, :], psT[:, :], ACT.Copy).then_inc(sig("qsmT_ready"), 1)
                slope(7)
                if norm2 and attn:
                    feature_major_norm2()
            slots(act, slot)

        @block.vector
        def _(dve):
            def tile_statistics(norm, name, src, tiles=range(NT)):
                for t in tiles:
                    last = nc.vector.bn_stats(st[:, norm, t, :], src(t))
                last.then_inc(sig(name + "_st"), 1)

            def token_statistics(norm, name, st_count, count):
                dve.wait_ge(sig(name + "_st"), st_count)
                nc.vector.tensor_tensor(negmean[:, norm, :], st[:, norm, :, 1], st[:, norm, :, 4], ALU.add)
                nc.vector.tensor_tensor(sdiff[:, norm, :], st[:, norm, :, 1], st[:, norm, :, 4], ALU.subtract)
                nc.vector.tensor_tensor(sdev[:, norm, :], st[:, norm, :, 2], st[:, norm, :, 5], ALU.add) \
                    .then_inc(sig(name + "_sum"), 1)
                dve.wait_ge(sig(name + "_sum"), count)
                nc.vector.tensor_tensor(sdiff[:, norm, :], sdiff[:, norm, :], sdiff[:, norm, :], ALU.mult)
                nc.vector.tensor_scalar(negmean[:, norm, :], negmean[:, norm, :], -0.5, None, ALU.mult)
                nc.vector.tensor_scalar(sdev[:, norm, :], sdev[:, norm, :], 1.0 / D, EPS, ALU.mult, ALU.add) \
                    .then_inc(sig(name + "_sq"), 1)
                dve.wait_ge(sig(name + "_sq"), count)
                nc.vector.scalar_tensor_tensor(veps[:, norm, :], sdiff[:, norm, :], 0.25, sdev[:, norm, :],
                                               ALU.mult, ALU.add).then_inc(sig(name + "_var"), 1)

            def input_statistics(b, half):
                tile_statistics(b % 2, "in", lambda t: xb(xraw, b, t * P, P), range(4 * half, 4 * half + 4))

            def input_variances(b):
                wait(dve, "in_shift", b - 1)
                token_statistics(b % 2, "in", 2 * b + 2, b + 1)

            def split_input(b, half):
                cols = slice(half * HALF, (half + 1) * HALF)
                src = expert_tokens(b)
                wait(dve, "experts_done", 2 * NT * (b - 1) + NT * (half + 1))
                dve.wait_ge(sig("xn0T_ready"), b + 1)
                nc.vector.tensor_copy(xn2_hi[:, cols], src[:, cols]).then_inc(sig("xn0_hi_ready"), 1)
                dve.wait_ge(sig("xn0_hi_ready"), 2 * b + half + 1)
                nc.vector.tensor_tensor(xn2_lo[:, cols], src[:, cols], xn2_hi[:, cols].bitcast(F32),
                                        ALU.subtract).then_inc(sig("xn0_lo_ready"), 1)

            def route(b):
                dve.wait_ge(sig("logits_done"), b + 1)
                nc.vector.tensor_tensor(lg[:, :, :], psS[:, 0:NT * E].rearrange("p (t e) -> p t e", e=E),
                                        rb_bc[:, :].unsqueeze(1).broadcast_to([P, NT, E]), ALU.add) \
                    .then_inc(sig("lg_ready"), 1)
                dve.wait_ge(sig("lg_ready"), b + 1)
                nc.vector.tensor_reduce(lmax[:, :], lg[:, :, :], AX_X, ALU.max).then_inc(sig("lmax_ready"), 1)
                dve.wait_ge(sig("lmax_ready"), b + 1)
                nc.vector.tensor_tensor(eq[:, :, :], lg[:, :, :],
                                        lmax[:, :].unsqueeze(2).broadcast_to([P, NT, E]), ALU.is_equal) \
                    .then_inc(sig("eq_ready"), 1)
                nc.vector.tensor_tensor(lg[:, :, :], lg[:, :, :],
                                        lmax[:, :].unsqueeze(2).broadcast_to([P, NT, E]), ALU.subtract) \
                    .then_inc(sig("lsub_ready"), 1)
                dve.wait_ge(sig("eq_ready"), b + 1)
                nc.vector.tensor_tensor(eq[:, :, :], eq[:, :, :],
                                        rank[:, :].unsqueeze(1).broadcast_to([P, NT, E]), ALU.mult) \
                    .then_inc(sig("score_ready"), 1)
                dve.wait_ge(sig("score_ready"), b + 1)
                nc.vector.tensor_reduce(lmax2[:, :], eq[:, :, :], AX_X, ALU.max).then_inc(sig("lmax2_ready"), 1)
                dve.wait_ge(sig("lmax2_ready"), b + 1)
                nc.vector.tensor_tensor(eq[:, :, :], eq[:, :, :],
                                        lmax2[:, :].unsqueeze(2).broadcast_to([P, NT, E]), ALU.is_equal) \
                    .then_inc(sig("first_ready"), 1)

            def pick_weight(b):
                dve.wait_ge(sig("lexp_ready"), b + 1)
                nc.vector.tensor_reduce(lsum[:, :], le[:, :, :], AX_X, ALU.add).then_inc(sig("lsum_ready"), 1)
                dve.wait_ge(sig("lsum_ready"), b + 1)
                nc.vector.reciprocal(lrec[:, :], lsum[:, :]).then_inc(sig("lrec_ready"), 1)
                dve.wait_ge(sig("first_ready"), b + 1)
                dve.wait_ge(sig("lrec_ready"), b + 1)
                wait(dve, "pickT_done", b - 1)
                wait(dve, "picked_act", NT * (b - 1))
                nc.vector.tensor_tensor(pick[:, b % 2, :, :], eq[:, :, :],
                                        lrec[:, :].unsqueeze(2).broadcast_to([P, NT, E]), ALU.mult) \
                    .then_inc(sig("pick_ready"), 1)
                dve.wait_ge(sig("pick_ready"), b + 1)

            def add_bias(b, half):
                dve.wait_ge(sig("ebias_done"), 2 * b + half + 1)
                dve.wait_ge(sig("pool_summed"), pool_sums(b, 4 * half + 3))
                dve.wait_ge(sig("dve_summed"), dve_sums(b, 4 * half + 3))
                nc.vector.tensor_tensor(xb(gate, b, half * HALF, HALF), xb(gate, b, half * HALF, HALF), psY[:, :],
                                        ALU.add).then_inc(sig("bias_added"), 1)

            def expert_step(b, t):
                dve.wait_ge(sig("experts_done"), 2 * NT * b + 2 * t + 1)
                if NT * b + t >= NBUF:
                    name, count = summed_before(b, t)
                    dve.wait_ge(sig(name), count)
                nc.vector.tensor_tensor(
                    ebuf[:, t % NBUF, 0:4, :],
                    expert_bank(b, t, 0).rearrange("p (e d) -> p e d", d=D),
                    pick[:, b % 2, t, 0:4].unsqueeze(2).broadcast_to([P, 4, D]), ALU.mult) \
                    .then_inc(sig("picked_dve"), 1)
                if t in DVE_SUM[b]:
                    dve.wait_ge(sig("picked_dve"), NT * b + t + 1)
                    dve.wait_ge(sig("picked_act"), NT * b + t + 1)
                    nc.vector.tensor_reduce(xb(gate, b, t * P, P),
                                            ebuf[:, t % NBUF, :, :].rearrange("p e d -> p d e"), AX_X, ALU.add) \
                        .then_inc(sig("dve_summed"), 1)
                if t in (2, 4) and b > 0:
                    add_bias(b - 1, t // 2 - 1)
                if t == 0 and b > 0:
                    split_input(b, 1)
                if t == 5 and b < NBATCH - 1:
                    split_input(b + 1, 0)
                if t == 6:
                    dve.wait_ge(sig("pickT_done"), b + 1)
                    nc.vector.tensor_copy(pickT[:, :], psY[0:NT * E, 0:P]).then_inc(sig("pickT_ready"), 1)

            def normalise_rest(item, batch, par):
                dve.wait_ge(sig("ln1_shift"), item + 1)
                wait(dve, "g_done", item - 1)
                for t in range(4, 8):
                    last = nc.vector.tensor_scalar(tile(xh1[:, par, :], t), xb(X, batch, t * P, P),
                                                   rstd[:, 0, t:t + 1], shift[:, 0, t:t + 1], ALU.mult, ALU.add)
                last.then_inc(sig("xh1b_ready"), 1)

            def norm1_half(batch, half):
                tile_statistics(0, "ln1", lambda t: xb(X, batch, t * P, P), range(4 * half, 4 * half + 4))

            dve.wait_ge(sig("x_first_loaded"), 16)
            input_statistics(0, 0)
            input_statistics(0, 1)
            input_variances(0)
            dve.wait_ge(sig("x_loaded"), 16 * (NBATCH - 1))
            input_statistics(1, 0)
            input_statistics(1, 1)
            input_variances(1)
            nc.vector.memset(ones[:, :], 1.0)
            nc.vector.memset(eighth[:, :], 1.0 / H).then_inc(sig("ones_ready"), 1)
            dve.wait_ge(sig("ew_hi_ready"), 1)
            nc.vector.tensor_tensor(ew_lo[:, :, :], ewn[:, :, :], ew_hi[:, :, :].bitcast(F32), ALU.subtract) \
                .then_inc(sig("ew_split"), 1)
            split_input(0, 0)
            split_input(0, 1)
            dve.wait_ge(sig("ones_ready"), 1)
            dve.wait_ge(sig("mask_ready"), 1)
            dve.wait_ge(sig("rank_ready"), E)
            dve.wait_ge(sig("router_loaded"), 32)
            route(0)
            pick_weight(0)
            for b in range(2):
                for t in range(NT):
                    expert_step(b, t)
                    if b == 0 and t == 0:
                        input_statistics(2, 0)
                        input_statistics(2, 1)
                        input_variances(2)
                    if b == 0 and t == 2:
                        input_statistics(3, 0)
                        input_statistics(3, 1)
                        input_variances(3)
                    if b == 0 and t == 4:
                        route(1)
                    if b == 0 and t == 6:
                        pick_weight(1)
                    if b == 1 and t == 2:
                        dve.wait_ge(sig("in_shift"), 3)
                        norm1_half(0, 0)
                        norm1_half(0, 1)
                        token_statistics(0, "ln1", 2, 1)
                    if b == 1 and t == 4:
                        route(2)
                    if b == 1 and t == 5:
                        pick_weight(2)
                    if b == 1 and t == 6:
                        dve.wait_ge(sig("x0_ready"), 3)
                        normalise_rest(0, 0, 0)
            route(3)

            def stage_w1(l):
                wait(dve, "h_done", NF * (4 * l))
                nc.vector.tensor_copy(w1_hi[:, :, :],
                                      of_layer(w1_all, l, 0, FF).rearrange("p (m c) -> p c m", c=NC)) \
                    .then_inc(sig("w1_hi_ready"), 1)

            def add_y(f, batch, half):
                dve.wait_ge(sig("y_done"), 2 * f + half + 1)
                nc.vector.tensor_tensor(xb(X, batch, half * HALF, HALF), xb(X, batch, half * HALF, HALF), psY[:, :],
                                        ALU.add).then_inc(sig("y_added"), 1)

            def gated(b, half=None):
                cols = slice(0, T) if half is None else slice(half * HALF, (half + 1) * HALF)
                dve.wait_ge(sig("gate_ready"), b + 1)
                dve.wait_ge(sig("y_added"), 2 * (4 * L - NBATCH + b) + (2 if half is None else half + 1))
                nc.vector.tensor_tensor(gate[:, b, cols], gate[:, b, cols], X[:, b, cols], ALU.mult) \
                    .then_inc(sig("gated"), 1)
                if half is not None:
                    dve.wait_ge(sig("gated"), NBATCH + half)
                    nc.vector.tensor_tensor(xraw[:, b, cols], xraw[:, b, cols], gate[:, b, cols], ALU.add) \
                        .then_inc(sig("last_out_ready"), 1)

            def slot(l, j):
                (attn, _), (norm2, _), (ffn, lf) = items(l, j)
                n = 4 * l + j
                f = n - 2
                par = j % 2
                fbatch = (j - 2) % 4
                nbatch = (j - 1) % 4

                def leaky(i):
                    if ffn:
                        dve.wait_ge(sig("hsl_ready"), NF * f + i + 1)
                        nc.vector.tensor_tensor(hid[:, i % NC, :], psH[:, i % 2, :], hsl[:, i % 2, :], ALU.max) \
                            .then_inc(sig("hid_ready"), 1)
                    elif attn:
                        expert_step(n + 2, i)

                def high_part(f):
                    dve.wait_ge(sig("xn2_ready"), f + 1)
                    nc.vector.tensor_copy(parts(f)[0], xn2[:, :]).then_inc(sig("xn2_hi_ready"), 1)

                if attn and j == 0:
                    wait(dve, "k_done", n)
                    wait(dve, "ctx_done", n)
                    wait(dve, "xnT_ready", n)
                    nc.vector.tensor_copy(lns[:, 0:1], param(0, l))
                    nc.vector.tensor_copy(lns[:, 1:2], param(1, l))
                    nc.vector.tensor_copy(wk_s[:, :], of_layer(wk_all, l, 0, D))
                    nc.vector.tensor_copy(wv_s[:, :], of_layer(wv_all, l, 0, D)).then_inc(sig("wkv_staged"), 1)
                if attn and j == 1:
                    wait(dve, "xn2_ready", n - 1)
                    nc.vector.tensor_copy(lns[:, 2:3], param(2, l))
                    nc.vector.tensor_copy(lns[:, 3:4], param(3, l)).then_inc(sig("ln2_staged"), 1)
                if not ffn or emptying(n, 1):
                    leaky(0)
                if ffn and not emptying(n, 1):
                    wait(dve, "h_done", NF * f)
                    high_part(f)
                if norm2:
                    dve.wait_ge(sig("attn_done"), n)
                    nc.vector.tensor_tensor(xb(X, nbatch), xb(X, nbatch), psM[:, :], ALU.add) \
                        .then_inc(sig("x1_added"), 1)
                if isinstance(n, int) and n == 2:
                    add_bias(NBATCH - 1, 1)
                last_ffn = 4 * l + j - 3
                if not isinstance(last_ffn, int) or last_ffn >= 0:
                    add_y(last_ffn, (j - 3) % 4, 1)
                if emptying(n, 0):
                    leaky(0)
                if norm2:
                    dve.wait_ge(sig("x1_added"), n)
                    tile_statistics(1, "ln2", lambda t: xb(X, nbatch, t * P, P))
                if ffn and not emptying(n, 1):
                    leaky(1 if emptying(n, 0) else 0)
                if norm2:
                    wait(dve, "ln2_shift", n - 1)
                    token_statistics(1, "ln2", n, n)
                if not ffn:
                    leaky(1)
                if isinstance(n, int) and n == 0:
                    pick_weight(3)
                if attn:
                    dve.wait_ge(sig("k_done"), n + 1)
                    nc.vector.tensor_reduce(negkmax[:, par:par + 1], psT[:, :], AX_X, ALU.max, negate=True) \
                        .then_inc(sig("negkmax_ready"), 1)
                if ffn and not emptying(n, 0):
                    leaky(1)
                if attn:
                    dve.wait_ge(sig("q_done"), n + 1)
                    nc.vector.tensor_reduce(qmax[:, :], by_head(psM[:, :]), AX_X, ALU.max) \
                        .then_inc(sig("qmax_ready"), 1)
                leaky(2)
                if emptying(n, 1):
                    gated(1)
                if attn:
                    if j == 0:
                        dve.wait_ge(sig("bv_done"), l + 1)
                        nc.vector.tensor_scalar(bvm[:, :], ones[:, :], psS[:, 0:1], 1.0 / H, ALU.mult, ALU.mult) \
                            .then_inc(sig("bv_ready"), 1)
                    dve.wait_ge(sig("qmax_ready"), n + 1)
                    wait(dve, "qsm_ready", n)
                    nc.vector.tensor_tensor(by_head(qe[:, :]), by_head(psM[:, :]), over_head(qmax[:, :]),
                                            ALU.subtract).then_inc(sig("qe_ready"), 1)
                    if j == 0:
                        dve.wait_ge(sig("bias_done"), l + 1)
                        nc.vector.tensor_copy(bias_row[:, :], psS[:, 0:D]).then_inc(sig("bias_ready"), 1)
                if not ffn:
                    leaky(3)
                if norm1_next(l, j):
                    wait(dve, "y_added", 2 * (n - 3) + 2)
                    norm1_half((j + 1) % 4, 1)
                if ffn:
                    leaky(3)
                if emptying(n, 0):
                    dve.wait_ge(sig("ln2_shift"), n)
                    wait(dve, "t2_done", n - 1)
                    for t in range(4, 8):
                        last = nc.vector.tensor_scalar(tile(xh2, t), xb(X, nbatch, t * P, P),
                                                       rstd[:, 1, t:t + 1], shift[:, 1, t:t + 1], ALU.mult, ALU.add)
                    last.then_inc(sig("xh2b_ready"), 1)
                if norm1_next(l, j):
                    dve.wait_ge(sig("ln1_shift"), n + 1)
                    token_statistics(0, "ln1", 2 * n + 4, n + 2)
                if attn:
                    dve.wait_ge(sig("expq_ready"), n + 1)
                    nc.vector.tensor_reduce(qsum[:, :], by_head(qe[:, :]), AX_X, ALU.add) \
                        .then_inc(sig("qsum_ready"), 1)
                leaky(4)
                if attn:
                    dve.wait_ge(sig("qsum_ready"), n + 1)
                    nc.vector.reciprocal(qrec[:, :], qsum[:, :]).then_inc(sig("qrec_ready"), 1)
                    nc.vector.reciprocal(krec[:, :], ksum[:, par:par + 1]).then_inc(sig("krec_ready"), 1)
                    dve.wait_ge(sig("g_done"), n + 1)
                    nc.vector.tensor_scalar(gT[:, :], psS[:, 0:D], lns[:, 0:1], None, ALU.mult) \
                        .then_inc(sig("gT_ready"), 1)
                if emptying(n, 0):
                    gated(0)
                if ffn:
                    add_y(f, fbatch, 0)
                if emptying(n, 1):
                    gated(2)
                if not ffn:
                    leaky(5)
                if attn:
                    dve.wait_ge(sig("ctx_done"), n + 1)
                    nc.vector.tensor_tensor(ctxT[:, :], psS[:, 0:D], head_mask[:, :], ALU.mult) \
                        .then_inc(sig("ctx_ready"), 1)
                if ffn:
                    leaky(5)
                if emptying(n, 0):
                    high_part(n - 1)
                leaky(6)
                if attn:
                    dve.wait_ge(sig("mix_done"), n + 1)
                    dve.wait_ge(sig("krec_ready"), n + 1)
                    nc.vector.scalar_tensor_tensor(mix[:, :], psS[:, 0:D], krec[:, 0:1], bias_row[:, :],
                                                   ALU.mult, ALU.add).then_inc(sig("mix_ready"), 1)
                if isinstance(n, int) and n == 0:
                    dve.wait_ge(sig("x0_ready"), NBATCH)
                if norm1_next(l, j):
                    normalise_rest(n + 1, (j + 1) % 4, (j + 1) % 2)
                leaky(7)
                if not isinstance(n, int) or n + 2 < 4 * L:
                    wait(dve, "y_added", 2 * (n - 2) + 1)
                    norm1_half((j + 2) % 4, 0)
                if isinstance(n, int) and n == 1:
                    add_bias(NBATCH - 1, 0)
                if emptying(n, 1):
                    gated(NBATCH - 1, 0)
                if attn and j == (0 if isinstance(n, int) else 1):
                    stage_w1(l)

            dve.wait_ge(sig("param_loaded"), 16 * 2)
            dve.wait_ge(sig("attn_loaded"), 16 * 4 * L)
            dve.wait_ge(sig("ffn_loaded"), 16 * 2 * L)
            dve.wait_ge(sig("x0_ready"), 2)
            norm1_half(1, 0)
            slots(dve, slot)
            add_y(4 * L - 1, 3, 1)
            gated(NBATCH - 1, 1)

        @block.gpsimd
        def _(pool):
            nc.gpsimd.memset(ident[:, :], 0.0).then_inc(sig("const_ready"), 1)
            nc.gpsimd.memset(head_mask[:, :], 1.0).then_inc(sig("const_ready"), 1)
            nc.gpsimd.memset(minus_half[:, :], -0.5).then_inc(sig("const_ready"), 1)
            nc.gpsimd.memset(eb_diag[:, :, :], 0.0).then_inc(sig("eb_zeroed"), 1)
            pool.wait_ge(sig("const_ready"), 3)
            nc.gpsimd.affine_select(out=ident[:, :], in_=ident[:, :], compare_op=ALU.not_equal, fill=1.0, base=0,
                                    pattern=[[-1, P]], channel_multiplier=1).then_inc(sig("const_ready"), 1)
            by = head_mask[:, :].rearrange("p (g d) -> p g d", d=DH)
            nc.gpsimd.affine_select(out=by, in_=by, compare_op=ALU.is_ge, fill=0.0, base=0,
                                    pattern=[[-DH, H], [0, DH]], channel_multiplier=1) \
                .then_inc(sig("mask_step"), 1)
            pool.wait_ge(sig("mask_step"), 1)
            nc.gpsimd.affine_select(out=by, in_=by, compare_op=ALU.is_ge, fill=0.0, base=DH - 1,
                                    pattern=[[DH, H], [0, DH]], channel_multiplier=-1) \
                .then_inc(sig("mask_ready"), 1)
            for e in range(E):
                nc.gpsimd.memset(rank[:, e:e + 1], float(E - e)).then_inc(sig("rank_ready"), 1)

            def reciprocal_deviations(norm, name, count):
                pool.wait_ge(sig(name + "_var"), count)
                nc.gpsimd.tensor_tensor(rstd[:, norm, :], veps[:, norm, :], minus_half[:, :], ALU.pow) \
                    .then_inc(sig(name + "_rstd"), 1)
                pool.wait_ge(sig(name + "_rstd"), count)
                nc.gpsimd.tensor_tensor(shift[:, norm, :], negmean[:, norm, :], rstd[:, norm, :], ALU.mult) \
                    .then_inc(sig(name + "_shift"), 1)

            def expert_sum(b, t):
                pool.wait_ge(sig("picked_dve"), NT * b + t + 1)
                pool.wait_ge(sig("picked_act"), NT * b + t + 1)
                a = ebuf[:, t % NBUF, :, :]
                nc.gpsimd.tensor_tensor(a[:, 0:4, :], a[:, 0:4, :], a[:, 4:8, :], ALU.add) \
                    .then_inc(sig("sum4"), 1)
                pool.wait_ge(sig("sum4"), pool_sums(b, t))
                nc.gpsimd.tensor_tensor(a[:, 0:2, :], a[:, 0:2, :], a[:, 2:4, :], ALU.add) \
                    .then_inc(sig("sum2"), 1)
                pool.wait_ge(sig("sum2"), pool_sums(b, t))
                nc.gpsimd.tensor_tensor(xb(gate, b, t * P, P), a[:, 0, :], a[:, 1, :], ALU.add) \
                    .then_inc(sig("pool_summed"), 1)

            def split_w1(l):
                pool.wait_ge(sig("w1_hi_ready"), l + 1)
                nc.gpsimd.tensor_tensor(w1_lo[:, :, :],
                                        of_layer(w1_all, l, 0, FF).rearrange("p (m c) -> p c m", c=NC),
                                        w1_hi[:, :, :].bitcast(F32), ALU.subtract).then_inc(sig("w1_staged"), 1)

            def slot(l, j):
                (attn, _), (norm2, _), (ffn, _) = items(l, j)
                n = 4 * l + j
                f = n - 2

                def low_part(f):
                    pool.wait_ge(sig("xn2_hi_ready"), f + 1)
                    hi, lo = parts(f)
                    for h in range(2):
                        cols = slice(h * HALF, (h + 1) * HALF)
                        nc.gpsimd.tensor_tensor(lo[:, cols], xn2[:, cols], hi[:, cols].bitcast(F32),
                                                ALU.subtract).then_inc(sig("xn2_lo_ready"), 1)

                def sums(*tiles):
                    if attn and not ffn:
                        for t in tiles:
                            if t not in DVE_SUM[n + 2]:
                                expert_sum(n + 2, t)

                if ffn and not emptying(n, 1):
                    low_part(f)
                if norm2:
                    wait(pool, "xh2_ready", NT * (n - 1))
                    reciprocal_deviations(1, "ln2", n)
                if emptying(n, 0):
                    low_part(n - 1)
                sums(0, 1, 2)
                if norm1_next(l, j):
                    pool.wait_ge(sig("xh1a_ready"), 4 * (n + 1))
                    pool.wait_ge(sig("xh1b_ready"), n + 1)
                    reciprocal_deviations(0, "ln1", n + 2)
                if attn:
                    pool.wait_ge(sig("qrec_ready"), n + 1)
                    wait(pool, "tq_done", n)
                    nc.gpsimd.tensor_tensor(by_head(qsm[:, :]), by_head(qe[:, :]), over_head(qrec[:, :]), ALU.mult) \
                        .then_inc(sig("qsm_ready"), 1)
                sums(3, 4, 5, 6, 7)
                if attn and j == (0 if isinstance(n, int) else 1):
                    split_w1(l)

            reciprocal_deviations(0, "in", 1)
            reciprocal_deviations(1, "in", 2)
            pool.wait_ge(sig("xh0_ready"), 1)
            reciprocal_deviations(0, "in", 3)
            for b in range(2):
                for t in range(NT):
                    if t not in DVE_SUM[b]:
                        expert_sum(b, t)
                    if b == 0 and t == 2:
                        pool.wait_ge(sig("xh0_ready"), 2)
                        reciprocal_deviations(1, "in", 4)
                    if b == 1 and t == 2:
                        pool.wait_ge(sig("xh0_ready"), 3)
                        reciprocal_deviations(0, "ln1", 1)
            slots(pool, slot)
            for b in range(NBATCH - 1):
                pool.wait_ge(sig("gated"), b + 1)
                nc.gpsimd.tensor_tensor(xraw[:, b, :], xraw[:, b, :], gate[:, b, :], ALU.add) \
                    .then_inc(sig("out_ready"), 1)


_OUTS = [((4, 1024, 128), 'float32')]


def kernel(**inputs):
    import numpy as _np
    import concourse.bacc as _bacc
    from concourse import mybir as _mybir
    from concourse.bass_utils import run_bass_kernel_spmd as _run

    a = {k[3:]: _np.asarray(v) for k, v in inputs.items()}
    laid_out = {
        "x": a["attn_x"],
        "ln_params": _np.stack([a[f"attn_{k}"].T for k in ("ln1_w", "ln1_b", "ln2_w", "ln2_b")], axis=1),
        "wq": a["attn_wq"], "wk": a["attn_wk"], "wv": a["attn_wv"], "wo": a["attn_wo"], "bo": a["attn_bo"],
        "w1": a["attn_w1"], "w2": a["attn_w2"],
        "router_wT": a["ffn_router_w"].T, "router_b": a["ffn_router_b"],
        "expert_wT": a["ffn_expert_w"].transpose(2, 0, 1), "expert_b": a["ffn_expert_b"],
    }
    nc = _bacc.Bacc("TRN2", target_bir_lowering=False, num_devices=1)
    arrays, args = {}, []
    for name, value in laid_out.items():
        value = _np.ascontiguousarray(value)
        arrays[f"in_{name}_dram"] = value
        args.append(nc.dram_tensor(f"in_{name}_dram", value.shape, _mybir.dt.from_np(value.dtype),
                                   kind="ExternalInput").ap())
    for i, (shape, dtype) in enumerate(_OUTS):
        dt = _mybir.dt.from_np(_np.dtype(dtype))
        args.append(nc.dram_tensor(f"out_{i}_dram", shape, dt, kind="ExternalOutput").ap())
    build_program(nc, *args)
    r = _run(nc, [arrays], core_ids=[0])
    return r.results[0]["out_0_dram"]
```
